# Optimizing a Trainium2 kernel written in Bass

```python
import numpy as np
import jax
import jax.numpy as jnp

def _softmax(x, axis=-1):
    return jax.nn.softmax(x, axis=axis)

def _gelu(x):
    return jax.nn.gelu(x, approximate=True)

def _silu(x):
    return jax.nn.silu(x)

def _sigmoid(x):
    return jax.nn.sigmoid(x)

def _layernorm(x, axis=-1, eps=1e-05):
    m = jnp.mean(x, axis=axis, keepdims=True)
    v = jnp.var(x, axis=axis, keepdims=True)
    return (x - m) / jnp.sqrt(v + eps)

def _scatter_add(tgt, idx, src, axis=0):
    return tgt.at[idx].add(src)

def _segment_sum(src, seg, n):
    return jax.ops.segment_sum(src, seg, n)
kernel_name = 'mk_xattn_ffn_d1_seqx_r8_b897d5'

def setup_inputs(seed: int=0):
    np.random.seed(seed)
    _w = jnp.asarray

    def _rec_inputs():
        import jax
        import jax.numpy as jnp
        _rk = jax.random.key(seed)
        x = -0.0001538 + 1 * jax.random.normal(jax.random.fold_in(_rk, 1), (32, 64, 128), jnp.float32)
        _lenS = 64 - jax.random.randint(jax.random.fold_in(_rk, 7), (32,), 0, max(1, 64 // 4) + 1, jnp.int32)
        _lenS2 = 64 - jax.random.randint(jax.random.fold_in(_rk, 8), (32,), 0, max(1, 64 // 4) + 1, jnp.int32)
        _ctx_1024P = jax.random.normal(jax.random.fold_in(_rk, 11), (32, 16, 128), jnp.float32)
        _ctx_1024c = jax.random.dirichlet(jax.random.fold_in(_rk, 511), 0.3 * jnp.ones((16,), jnp.float32), (32, 64))
        _ctx_1024t = jnp.einsum('bsk,bkd->bsd', _ctx_1024c, _ctx_1024P)
        _ctx_1024t = _ctx_1024t * jax.lax.rsqrt(jnp.mean(jnp.square(_ctx_1024t)) + 1e-12) * 0.953939
        ctx_1024 = -0.000191848 + 0.999787 * (_ctx_1024t + 0.3 * jax.random.normal(jax.random.fold_in(_rk, 611), (32, 64, 128), jnp.float32))
        return (x, ctx_1024)
    x, ctx_1024 = _rec_inputs()

    def _L0_xattn_setup():
        import jax, jax.numpy as jnp
        import numpy as np
        EMBED_DIM = 128
        NUM_HEADS = 16
        THETA = 10000.0

        def apply_rope(x):
            B, T, C = x.shape
            freqs = 1.0 / THETA ** (jnp.arange(0, C, 2, dtype=jnp.float32) / C)
            t = jnp.arange(T, dtype=jnp.float32)
            ang = jnp.outer(t, freqs)
            cosv, sinv = (jnp.cos(ang), jnp.sin(ang))
            xr = x.reshape(B, T, C // 2, 2)
            real = xr[..., 0] * cosv - xr[..., 1] * sinv
            imag = xr[..., 0] * sinv + xr[..., 1] * cosv
            return jnp.stack([real, imag], axis=-1).reshape(B, T, C)
        k = jax.random.key(seed)
        ks = jax.random.split(k, 7)
        B, T, C = (8, 96, EMBED_DIM)
        w_scale = 1.0 / np.sqrt(C)
        return {'query': jax.random.normal(ks[0], (B, T, C), jnp.float32), 'key': jax.random.normal(ks[1], (B, T, C), jnp.float32), 'value': jax.random.normal(ks[2], (B, T, C), jnp.float32), 'Wq': jax.random.normal(ks[3], (C, C), jnp.float32) * w_scale, 'Wk': jax.random.normal(ks[4], (C, C), jnp.float32) * w_scale, 'Wv': jax.random.normal(ks[5], (C, C), jnp.float32) * w_scale, 'Wo': jax.random.normal(ks[6], (C, C), jnp.float32) * w_scale}
    _L0_xattn_all = _L0_xattn_setup()
    _L0_xattn_in = {k: v for k, v in _L0_xattn_all.items() if k in ('Wq', 'Wk', 'Wv', 'Wo')}
    del _L0_xattn_all

    def _L0_ffn_setup():
        import jax, jax.numpy as jnp
        import numpy as np
        DIM = 128
        E = 16
        TOPK = 2
        G = 4
        TOPK_G = 2
        INTER = 64
        N_SHARED = 2
        ROUTE_SCALE = 1.0

        def _gate(xf, gate_w, gate_b):
            scores = xf @ gate_w.T
            scores = jax.nn.softmax(scores.astype(jnp.float32), axis=-1)
            orig = scores
            scores = scores + gate_b
            T = xf.shape[0]
            sg = scores.reshape(T, G, E // G)
            group_scores = jax.lax.top_k(sg, 2)[0].sum(-1)
            _, gidx = jax.lax.top_k(group_scores, TOPK_G)
            keep = jax.nn.one_hot(gidx, G).sum(axis=1) > 0
            sg = jnp.where(keep[:, :, None], sg, -jnp.inf)
            scores = sg.reshape(T, E)
            _, idx = jax.lax.top_k(scores, TOPK)
            weights = jnp.take_along_axis(orig, idx, axis=1)
            weights = (weights * ROUTE_SCALE).astype(xf.dtype)
            return (weights, idx)
        key = jax.random.key(seed)
        ks = jax.random.split(key, 16)
        s = lambda fan_in: 1.0 / np.sqrt(fan_in)
        inp = {'x': jax.random.normal(ks[0], (4, 128, DIM), dtype=jnp.float32), 'gate_w': jax.random.normal(ks[1], (E, DIM), dtype=jnp.float32) * s(DIM), 'gate_b': jnp.zeros((E,), dtype=jnp.float32), 'We1': jax.random.normal(ks[2], (E, DIM, INTER), dtype=jnp.float32) * s(DIM), 'be1': jnp.zeros((E, INTER), dtype=jnp.float32), 'We2': jax.random.normal(ks[3], (E, INTER, DIM), dtype=jnp.float32) * s(INTER), 'be2': jnp.zeros((E, DIM), dtype=jnp.float32), 'We3': jax.random.normal(ks[4], (E, DIM, INTER), dtype=jnp.float32) * s(DIM), 'be3': jnp.zeros((E, INTER), dtype=jnp.float32), 'ws1': jax.random.normal(ks[5], (DIM, N_SHARED * INTER), dtype=jnp.float32) * s(DIM), 'bs1': jnp.zeros((N_SHARED * INTER,), dtype=jnp.float32), 'ws2': jax.random.normal(ks[6], (N_SHARED * INTER, DIM), dtype=jnp.float32) * s(N_SHARED * INTER), 'bs2': jnp.zeros((DIM,), dtype=jnp.float32), 'ws3': jax.random.normal(ks[7], (DIM, N_SHARED * INTER), dtype=jnp.float32) * s(DIM), 'bs3': jnp.zeros((N_SHARED * INTER,), dtype=jnp.float32)}
        return inp
    _L0_ffn_all = _L0_ffn_setup()
    _L0_ffn_in = {k: v for k, v in _L0_ffn_all.items() if k in ('gate_w', 'gate_b', 'We1', 'be1', 'We2', 'be2', 'We3', 'be3', 'ws1', 'bs1', 'ws2', 'bs2', 'ws3', 'bs3')}
    del _L0_ffn_all
    return {'x': x, 'ctx_1024': ctx_1024, 'L0_xattn_Wq': _L0_xattn_in['Wq'], 'L0_xattn_Wk': _L0_xattn_in['Wk'], 'L0_xattn_Wv': _L0_xattn_in['Wv'], 'L0_xattn_Wo': _L0_xattn_in['Wo'], 'L0_ffn_gate_w': _L0_ffn_in['gate_w'], 'L0_ffn_gate_b': _L0_ffn_in['gate_b'], 'L0_ffn_We1': _L0_ffn_in['We1'], 'L0_ffn_be1': _L0_ffn_in['be1'], 'L0_ffn_We2': _L0_ffn_in['We2'], 'L0_ffn_be2': _L0_ffn_in['be2'], 'L0_ffn_We3': _L0_ffn_in['We3'], 'L0_ffn_be3': _L0_ffn_in['be3'], 'L0_ffn_ws1': _L0_ffn_in['ws1'], 'L0_ffn_bs1': _L0_ffn_in['bs1'], 'L0_ffn_ws2': _L0_ffn_in['ws2'], 'L0_ffn_bs2': _L0_ffn_in['bs2'], 'L0_ffn_ws3': _L0_ffn_in['ws3'], 'L0_ffn_bs3': _L0_ffn_in['bs3']}

def reference(x, ctx_1024, L0_xattn_Wq, L0_xattn_Wk, L0_xattn_Wv, L0_xattn_Wo, L0_ffn_gate_w, L0_ffn_gate_b, L0_ffn_We1, L0_ffn_be1, L0_ffn_We2, L0_ffn_be2, L0_ffn_We3, L0_ffn_be3, L0_ffn_ws1, L0_ffn_bs1, L0_ffn_ws2, L0_ffn_bs2, L0_ffn_ws3, L0_ffn_bs3):
    import jax
    import jax.numpy as jnp

    def _L0_xattn_ref(query, key, value, Wq, Wk, Wv, Wo):
        import jax, jax.numpy as jnp
        import numpy as np
        EMBED_DIM = 128
        NUM_HEADS = 16
        THETA = 10000.0

        def apply_rope(x):
            B, T, C = x.shape
            freqs = 1.0 / THETA ** (jnp.arange(0, C, 2, dtype=jnp.float32) / C)
            t = jnp.arange(T, dtype=jnp.float32)
            ang = jnp.outer(t, freqs)
            cosv, sinv = (jnp.cos(ang), jnp.sin(ang))
            xr = x.reshape(B, T, C // 2, 2)
            real = xr[..., 0] * cosv - xr[..., 1] * sinv
            imag = xr[..., 0] * sinv + xr[..., 1] * cosv
            return jnp.stack([real, imag], axis=-1).reshape(B, T, C)
        B, T, C = query.shape
        H = NUM_HEADS
        D = C // H
        q = jnp.einsum('btc,oc->bto', query, Wq)
        k = jnp.einsum('btc,oc->bto', key, Wk)
        v = jnp.einsum('btc,oc->bto', value, Wv)
        q = apply_rope(q)
        k = apply_rope(k)
        q = q.reshape(B, T, H, D).transpose(0, 2, 1, 3)
        k = k.reshape(B, T, H, D).transpose(0, 2, 1, 3)
        v = v.reshape(B, T, H, D).transpose(0, 2, 1, 3)
        scale = 1.0 / jnp.sqrt(jnp.asarray(D, dtype=q.dtype))
        scores = jnp.einsum('bhqd,bhkd->bhqk', q, k) * scale
        attn = jax.nn.softmax(scores, axis=-1)
        y = jnp.einsum('bhqk,bhkd->bhqd', attn, v)
        y = y.transpose(0, 2, 1, 3).reshape(B, T, C)
        return jnp.einsum('btc,oc->bto', y, Wo)

    def _L0_ffn_ref(x, gate_w, gate_b, We1, be1, We2, be2, We3, be3, ws1, bs1, ws2, bs2, ws3, bs3):
        import jax, jax.numpy as jnp
        import numpy as np
        DIM = 128
        E = 16
        TOPK = 2
        G = 4
        TOPK_G = 2
        INTER = 64
        N_SHARED = 2
        ROUTE_SCALE = 1.0

        def _gate(xf, gate_w, gate_b):
            scores = xf @ gate_w.T
            scores = jax.nn.softmax(scores.astype(jnp.float32), axis=-1)
            orig = scores
            scores = scores + gate_b
            T = xf.shape[0]
            sg = scores.reshape(T, G, E // G)
            group_scores = jax.lax.top_k(sg, 2)[0].sum(-1)
            _, gidx = jax.lax.top_k(group_scores, TOPK_G)
            keep = jax.nn.one_hot(gidx, G).sum(axis=1) > 0
            sg = jnp.where(keep[:, :, None], sg, -jnp.inf)
            scores = sg.reshape(T, E)
            _, idx = jax.lax.top_k(scores, TOPK)
            weights = jnp.take_along_axis(orig, idx, axis=1)
            weights = (weights * ROUTE_SCALE).astype(xf.dtype)
            return (weights, idx)
        shape = x.shape
        xf = x.reshape(-1, DIM)
        weights, idx = _gate(xf, gate_w, gate_b)
        combine = (jax.nn.one_hot(idx, E, dtype=xf.dtype) * weights[..., None]).sum(1)
        h1 = jnp.einsum('td,edi->tei', xf, We1) + be1
        h3 = jnp.einsum('td,edi->tei', xf, We3) + be3
        h = jax.nn.silu(h1) * h3
        yo = jnp.einsum('tei,eid->ted', h, We2) + be2
        y = jnp.einsum('te,ted->td', combine, yo)
        z = jax.nn.silu(xf @ ws1 + bs1) * (xf @ ws3 + bs3) @ ws2 + bs2
        return (y + z).reshape(shape)
    x = x + _L0_xattn_ref(_layernorm(x, axis=-1), ctx_1024, ctx_1024, L0_xattn_Wq, L0_xattn_Wk, L0_xattn_Wv, L0_xattn_Wo)
    x = x + _L0_ffn_ref(_layernorm(x, axis=-1), L0_ffn_gate_w, L0_ffn_gate_b, L0_ffn_We1, L0_ffn_be1, L0_ffn_We2, L0_ffn_be2, L0_ffn_We3, L0_ffn_be3, L0_ffn_ws1, L0_ffn_bs1, L0_ffn_ws2, L0_ffn_bs2, L0_ffn_ws3, L0_ffn_bs3)
    return x

_drawn_inputs = setup_inputs


def setup_inputs(seed=0):
    import zlib

    import numpy as np

    out = dict(_drawn_inputs(seed))
    spreads = {'L0_ffn_gate_b': (0.0, 0.1),
     'L0_ffn_be1': (0.0, 0.611),
     'L0_ffn_be2': (0.0, 0.392),
     'L0_ffn_be3': (0.0, 0.619),
     'L0_ffn_bs1': (0.0, 0.1),
     'L0_ffn_bs2': (0.0, 0.1),
     'L0_ffn_bs3': (0.0, 0.1)}
    factors = {}
    for name, (base, spread) in spreads.items():
        noise = np.random.default_rng([zlib.crc32(name.encode()), seed]).standard_normal(out[name].shape)
        drawn = base * np.exp(spread * noise) if base else spread * noise
        out[name] = jnp.asarray(drawn.astype(out[name].dtype))
    for name, factor in factors.items():
        out[name] = (out[name] * factor).astype(out[name].dtype)
    return out
```

```python
from contextlib import ExitStack

import concourse.bass as bass
from concourse import mybir

F32 = mybir.dt.float32
F32R = mybir.dt.float32r
F16 = mybir.dt.float16
ALU = mybir.AluOpType
ACT = mybir.ActivationFunctionType
X = mybir.AxisListType.X

P = 128
C = 128
B, S = 32, 64
H, D = 16, 8
E, I = 16, 64
NG, GE = 4, 4
TOK = B * S
T = TOK // P
BT = P // S
HQ = 4
NS = H // HQ
ROW = P // HQ
MROW = 3 * D
TG = 4
G = T // TG
NP = H // 2
VW = D + 1
VB = BT * 2 * VW
QR = 3
CH = 512
NC = TOK // CH
J = E * I // P + 1
JE = J - 1
CR = 3
LEAD = 5
EPS = 1e-5
BIG = 1e30
BIGGER = 1e32

A_WQ, A_WK, A_WV, A_COS, A_SIN, A_ID = 0, 128, 256, 384, 640, 896
A_N = 1024
B_WO, B_GW, B_GB, B_B1, B_B3, B_S2, B_LT, B_REV = 0, 128, 144, 160, 169, 178, 179, 195
B_N = 211
K_B2, K_SEL = 0, 128
K_N = 128 + JE * P


def program(nc, x, ctx_in, pack_a, pack_b, pack_k, w1, w3, w2, out):
    with ExitStack() as st:
        def sb(name, shape, dt=F32):
            return st.enter_context(nc.sbuf_tensor(name, shape, dt))

        def sem(name):
            return st.enter_context(nc.semaphore(name))

        xs = sb("xs", [P, T, C])
        pa = sb("pa", [P, A_N])
        pb = sb("pb", [P, B_N])
        pk = sb("pk", [2 * E, K_N])
        sel_r = sb("sel_r", [2 * E, JE * P], F32R)
        b2h = sb("b2h", [2 * E, C], F32R)
        b2l = sb("b2l", [2 * E, C], F32R)
        gwh = sb("gwh", [P, E], F32R)
        gwl = sb("gwl", [P, E], F32R)
        ident16 = sb("ident16", [P, P], F16)
        eps_t = sb("eps_t", [P, 1])
        stat = sb("stat", [P, T, 6])
        mv = sb("mv", [P, T, 2])
        rstd = sb("rstd", [P, T])
        stat2 = sb("stat2", [P, T, 6])
        mv2 = sb("mv2", [P, T, 2])
        rstd2 = sb("rstd2", [P, T])
        mhalf = sb("mhalf", [P, T])
        Vh = sb("Vh", [P, T, NP, VB], F16)
        Vl = sb("Vl", [P, T, NP, VB], F16)
        x2h = sb("x2h", [P, TOK], F32R)
        x2l = sb("x2l", [P, TOK], F32R)
        wh = [sb(f"w{n}h", [P, J * P], F32R) for n in (1, 3, 2)]
        wl = [sb(f"w{n}l", [P, J * P], F32R) for n in (1, 3, 2)]
        mx = sb("mx", [P, G, 2 * NS * TG * BT])
        mneg = sb("mneg", [2 * NS * TG * BT, G, P], F16)
        rsum = sb("rsum", [P, 2, NP * BT])
        yt = sb("yt", [P, 2, C])
        yT = sb("yT", [P, 2, P])
        x2n = sb("x2n", [P, 2, C])
        x2f = sb("x2f", [P, 2, P])
        shared = sb("shared", [P, 4096])
        wraw = [shared[:, n * J * P:(n + 1) * J * P] for n in range(3)]
        P32 = shared[:, 0:2048].rearrange("p (s m) -> p s m", s=2)
        Ph = shared[:, 2048:3072].bitcast(F16).rearrange("p (s m) -> p s m", s=2)
        Pl = shared[:, 3072:4096].bitcast(F16).rearrange("p (s m) -> p s m", s=2)
        stk = sb("stk", [P, 2, G, NS, TG * P], F16)

        with ExitStack() as early:
            def eb(name, shape, dt=F32):
                return early.enter_context(nc.sbuf_tensor(name, shape, dt))

            QM = eb("QM", [P, QR, NS * TG * BT, HQ, S], F16)
            cs = eb("cs", [P, CR * TG, C])
            xh = eb("xh", [P, 2, C])
            xcT = eb("xcT", [P, 2, 2 * P])
            rt = eb("rt", [P, 2, 2, 2 * C])
            rs = eb("rs", [P, 2, 2 * C])
            EXW = 2 * NS * P
            ex = eb("ex", [P, 2, EXW], F16)
        sil = sb("sil", [P, 2, CH])
        U = sb("U", [P, 2, CH])
        G32 = sb("G32", [P, 2, CH])
        Gh = sb("Gh", [P, 3, CH], F32R)
        Gl = sb("Gl", [P, 3, CH], F32R)
        yo = sb("yo", [P, 2, CH])
        ob = sb("ob", [P, 2, CH])
        cT = sb("cT", [2 * E, TOK], F32R)
        gt = [sb(f"gt{n}", [P, T, E]) for n in range(10)]
        pair = [sb(f"pair{n}", [P, T * NG, 2]) for n in range(2)]
        gs = [sb(f"gs{n}", [P, T * NG]) for n in range(6)]
        tt = [sb(f"tt{n}", [P, T]) for n in range(8)]
        cc = sb("cc", [P, T, 2 * E], F32R)

        ps = st.enter_context(nc.psum_tensor("ps", [P, 8, 512], F32))

        def bank(n):
            return ps[:, n, :]

        wq = pa[:, A_WQ:A_WQ + C]
        wk = pa[:, A_WK:A_WK + C]
        wv = pa[:, A_WV:A_WV + C]
        cos = pa[:, A_COS:A_COS + 2 * C]
        sin = pa[:, A_SIN:A_SIN + 2 * C]
        ident = pa[:, A_ID:A_ID + P]
        wo = pb[:, B_WO:B_WO + C]
        gb = pb[:, B_GB:B_GB + E]
        below = pb[:, B_LT:B_LT + NG * NG]
        rev = pb[:, B_REV:B_REV + E]

        loaded_a = sem("loaded_a")
        loaded_b = sem("loaded_b")
        loaded_k = sem("loaded_k")
        loaded_x = [sem(f"loaded_x{g}") for g in range(G)]
        loaded_c = [sem(f"loaded_c{g}") for g in range(G)]
        loaded_w = [sem(f"loaded_w{n}") for n in range(3)]
        qm_zero = sem("qm_zero")
        ex_zero = sem("ex_zero")
        v_zero = sem("v_zero")
        consts = sem("consts")
        stats = sem("stats")
        mv_ready = sem("mv_ready")
        aggrs = sem("aggrs")
        rstds = sem("rstds")
        xh_ready = sem("xh_ready")
        T_done = sem("T_done")
        xcT_ready = sem("xcT_ready")
        qkv_done = sem("qkv_done")
        rot_done = sem("rot_done")
        rs_ready = sem("rs_ready")
        hi_ready = sem("hi_ready")
        lo_ready = sem("lo_ready")
        vh_ready = sem("vh_ready")
        vl_ready = sem("vl_ready")
        stackT_done = sem("stackT_done")
        stk_ready = sem("stk_ready")
        qm_loaded = [sem(f"qm_loaded{g}") for g in range(G)]
        id16_ready = sem("id16_ready")
        S_done = sem("S_done")
        mx_ready = sem("mx_ready")
        tm_done = sem("tm_done")
        tm_read = sem("tm_read")
        m_moved = [sem(f"m_moved{g}") for g in range(G)]
        ST_done = sem("ST_done")
        exp_ready = sem("exp_ready")
        ph_ready = sem("ph_ready")
        pl_ready = sem("pl_ready")
        pv_done = sem("pv_done")
        rsum_ready = sem("rsum_ready")
        yt_ready = sem("yt_ready")
        wo_done = sem("wo_done")
        x1_ready = sem("x1_ready")
        st2 = sem("st2")
        ag2 = sem("ag2")
        rstd2_ready = sem("rstd2_ready")
        x2n_ready = sem("x2n_ready")
        x2h_ready = sem("x2h_ready")
        x2l_ready = sem("x2l_ready")
        log_done = sem("log_done")
        wh_ready = sem("wh_ready")
        wl_ready = sem("wl_ready")
        gate_v = sem("gate_v")
        gate_e = sem("gate_e")
        cc_ready = sem("cc_ready")
        cT_done = sem("cT_done")
        cT_ready = sem("cT_ready")
        H1_done = sem("H1_done")
        H3_done = sem("H3_done")
        CR_done = sem("CR_done")
        sil_ready = sem("sil_ready")
        U_ready = sem("U_ready")
        G_ready = sem("G_ready")
        gh_ready = sem("gh_ready")
        gl_ready = sem("gl_ready")
        Y_part = sem("Y_part")
        yo_ready = sem("yo_ready")
        oT_done = sem("oT_done")
        ob_ready = sem("ob_ready")
        stored = [sem(f"stored{n}") for n in range(2)]

        UN = NC * J
        tm_uses = []
        steps2 = T + 8

        def max_tile(s):
            u = s + LEAD
            return u if u < T else None

        tm_uses.append(("m", 0))
        for s in range(steps2):
            if s + LEAD - 1 < T and (s + LEAD - 1) % TG == TG - 1 and (s + LEAD - 1) // TG > 0:
                tm_uses.append(("m", (s + LEAD - 1) // TG))
            if 0 <= s - 2 < T:
                tm_uses.append(("y", s - 2))
            if 0 <= s - 4 < T:
                tm_uses.append(("x", s - 4))
        tm_at = {use: n for n, use in enumerate(tm_uses)}

        x_v = x.rearrange("(g t p) c -> g p t c", g=G, p=P)
        c_v = ctx_in.rearrange("(g t p) c -> g p t c", g=G, p=P)
        o_v = out.rearrange("(n t p) c -> n p t c", n=NC, p=P)

        block = st.enter_context(nc.Block())

        @block.sync
        def _(sp):
            sp.dma_start(xs[:, 0:TG, :], x_v[0]).then_inc(loaded_x[0], 16)
            sp.dma_start(pa[:], pack_a).then_inc(loaded_a, 16)
            sp.dma_start(cs[:, 0:TG, :], c_v[0]).then_inc(loaded_c[0], 16)
            for g in range(1, G):
                sp.dma_start(xs[:, g * TG:(g + 1) * TG, :], x_v[g]).then_inc(loaded_x[g], 16)
                if g < CR:
                    sp.dma_start(cs[:, g * TG:(g + 1) * TG, :], c_v[g]).then_inc(loaded_c[g], 16)
            sp.dma_start(pb[:], pack_b).then_inc(loaded_b, 16)
            sp.dma_start(pk[:], pack_k).then_inc(loaded_k, 16)
            for n, w in enumerate((w1, w3, w2)):
                sp.dma_start(wraw[n], w).then_inc(loaded_w[n], 16)

            for g in range(CR, G):
                sp.wait_ge(T_done, (g - CR + 1) * TG)
                sp.dma_start(cs[:, (g - CR) * TG:(g - CR + 1) * TG, :], c_v[g]).then_inc(loaded_c[g], 16)

            def load_qm(g):
                sp.wait_ge(stk_ready, (g + 1) * TG)
                if g == 0:
                    sp.wait_ge(qm_zero, QR)
                if g >= QR:
                    sp.wait_ge(ST_done, 2 * TG * (g - QR + 1))
                for r in range(HQ):
                    rows = slice(ROW * r, ROW * r + ROW)
                    sp.dma_start(QM[rows, g % QR, :, r, :],
                                 stk[rows, 0, g].rearrange("p s (m q) -> p (s m) q", q=S)) \
                        .then_inc(qm_loaded[g], 16)

            def move_m(g):
                sp.wait_ge(tm_read, tm_at["m", g] + 1)
                half = NS * TG * BT
                for r in range(HQ):
                    rh, r2 = divmod(r, 2)
                    row = ROW * r + MROW
                    sp.dma_start(QM[row:row + 1, g % QR, :, r, :], mneg[half * rh:half * rh + half, g, S * r2:S * r2 + S]) \
                        .then_inc(m_moved[g], 16)

            for g in range(QR):
                load_qm(g)
            move_m(0)
            move_m(1)
            for g in range(QR, G):
                load_qm(g)
                move_m(g - 1)
            move_m(G - 1)
            for n in range(NC):
                sp.wait_ge(ob_ready, n + 1)
                sp.dma_start(o_v[n], ob[:, n % 2, :].rearrange("p (t c) -> p t c", c=C)) \
                    .then_inc(stored[n % 2], 16)
            for n in range(2):
                sp.wait_ge(stored[n], 16 * (NC // 2))

        @block.gpsimd
        def _(pool):
            g_ = nc.gpsimd
            g_.memset(mhalf[:], -0.5).then_inc(consts, 1)
            g_.memset(Vh[:].rearrange("p t n w -> p (t n w)").bitcast(F32), 0.0).then_inc(v_zero, 1)
            g_.memset(Vl[:].rearrange("p t n w -> p (t n w)").bitcast(F32), 0.0).then_inc(v_zero, 1)
            for b in range(BT):
                pool.wait_ge(v_zero, 2 + b)
                ones = Vh[S * b:S * b + S].rearrange("p t n (b h w) -> p (t n) b h w", b=BT, w=VW)
                g_.memset(ones[:, :, b, :, D], 1.0).then_inc(v_zero, 1)
            pool.wait_ge(v_zero, 2 + BT)

            def deviations(g):
                pool.wait_ge(consts, 1)
                pool.wait_ge(aggrs, (g + 1) * TG)
                a = mv[:, g * TG:(g + 1) * TG, 1]
                g_.tensor_tensor(rstd[:, g * TG:(g + 1) * TG], a, mhalf[:, 0:TG], ALU.pow).then_inc(rstds, 1)

            deviations(0)
            for q in range(1, QR):
                g_.memset(QM[:, q].rearrange("p m h q -> p (m h q)").bitcast(F32), 0.0).then_inc(qm_zero, 1)
            for s in range(T + 2):
                if s % TG == 1 and s // TG + 1 < G:
                    deviations(s // TG + 1)
                i = s - 1
                if 0 <= i < T:
                    pool.wait_ge(rot_done, 2 * (i + 1))
                    if i >= 2:
                        pool.wait_ge(lo_ready, 2 * (i - 1))
                    g_.tensor_tensor(rs[:, i % 2], rt[:, i % 2, 0], rt[:, i % 2, 1], ALU.add) \
                      .then_inc(rs_ready, 1)
                i = s - 2
                if 0 <= i < T:
                    pool.wait_ge(hi_ready, i + 1)
                    pool.wait_ge(rs_ready, i + 1)
                    o = ex[:, i % 2].rearrange("p (s h w) -> p s h w", s=2, w=ROW)
                    src = rs[:, i % 2].rearrange("p (s h w) -> p s h w", s=2, w=D)
                    g_.tensor_tensor(o[:, 0, :, 0:D], src[:, 0], o[:, 0, :, D:2 * D], ALU.subtract) \
                      .then_inc(lo_ready, 1)
                    g_.tensor_tensor(o[:, 1, :, 2 * D:3 * D], src[:, 1], o[:, 1, :, D:2 * D], ALU.subtract) \
                      .then_inc(lo_ready, 1)
            for n in (0, 1, 2):
                pool.wait_ge(wh_ready, n + 1)
                g_.tensor_tensor(wl[n][:], wraw[n], wh[n][:].bitcast(F32), ALU.subtract).then_inc(wl_ready, 1)
            pool.wait_ge(wh_ready, 5)
            g_.tensor_tensor(gwl[:], pb[:, B_GW:B_GW + E], gwh[:].bitcast(F32), ALU.subtract).then_inc(wl_ready, 1)
            g_.tensor_tensor(b2l[:], pk[:, K_B2:K_B2 + C], b2h[:].bitcast(F32), ALU.subtract).then_inc(wl_ready, 1)
            for s in range(steps2):
                if 0 <= s < T:
                    for hb in range(2):
                        u = 2 * s + hb
                        pool.wait_ge(ph_ready, u + 1)
                        if s >= 2:
                            pool.wait_ge(pv_done, s - 1)
                        c = slice(512 * hb, 512 * hb + 512)
                        g_.tensor_tensor(Pl[:, s % 2, c], P32[:, s % 2, c], Ph[:, s % 2, c], ALU.subtract) \
                          .then_inc(pl_ready, 1)
                i = s - 3
                if 0 <= i < T:
                    pool.wait_ge(ag2, i + 1)
                    g_.tensor_tensor(rstd2[:, i:i + 1], mv2[:, i, 1:2], mhalf[:, 0:1], ALU.pow) \
                      .then_inc(rstd2_ready, 1)
                i = s - 5
                if 0 <= i < T:
                    pool.wait_ge(x2h_ready, i + 1)
                    c = slice(P * i, P * i + P)
                    g_.tensor_tensor(x2l[:, c], x2f[:, i % 2], x2h[:, c].bitcast(F32), ALU.subtract) \
                      .then_inc(x2l_ready, 1)
            for u in range(UN):
                pool.wait_ge(gh_ready, u + 1)
                if u >= 3:
                    pool.wait_ge(Y_part, u - 2)
                g_.tensor_tensor(Gl[:, u % 3], G32[:, u % 2], Gh[:, u % 3].bitcast(F32), ALU.subtract) \
                  .then_inc(gl_ready, 1)

        @block.scalar
        def _(act):
            a_ = nc.scalar
            act.wait_ge(loaded_a, 16)
            a_.copy(ident16[:], ident).then_inc(id16_ready, 1)
            for s in range(T + 2):
                if s < T:
                    act.wait_ge(T_done, s + 1)
                    if s >= 2:
                        act.wait_ge(qkv_done, s - 1)
                    a_.copy(xcT[:, s % 2], bank(s % 2)[:, 0:2 * P]).then_inc(xcT_ready, 1)
                i = s - 1
                if 0 <= i < T:
                    act.wait_ge(qkv_done, i + 1)
                    if i == 0:
                        act.wait_ge(v_zero, 2 + BT)
                    for b in range(BT):
                        rows = slice(S * b, S * b + S)
                        src = bank(6 + i % 2)[rows, 0:C].rearrange("p (n h w) -> p n h w", h=2, w=D)
                        dst = Vh[rows, i].rearrange("p n (b h w) -> p n b h w", b=BT, w=VW)
                        a_.copy(dst[:, :, b, :, 0:D], src).then_inc(vh_ready, 1)
                    act.wait_ge(rs_ready, i + 1)
                    if i == 0:
                        act.wait_ge(ex_zero, 2)
                    if i >= 2:
                        act.wait_ge(stackT_done, i - 1)
                    o = ex[:, i % 2].rearrange("p (s h w) -> p s h w", s=2, w=ROW)
                    src = rs[:, i % 2].rearrange("p (s h w) -> p s h w", s=2, w=D)
                    for side, first in ((0, D), (1, 0)):
                        dst = o[:, side, :, first:first + 2 * D].rearrange("p h (k w) -> p h k w", k=2)
                        last = a_.copy(dst, src[:, side].unsqueeze(2).broadcast_to([P, H, 2, D]))
                    last.then_inc(hi_ready, 1)
            for n in range(3):
                act.wait_ge(loaded_w[n], 16)
                a_.copy(wh[n][:], wraw[n]).then_inc(wh_ready, 1)
            act.wait_ge(loaded_b, 16)
            a_.copy(gwh[:], pb[:, B_GW:B_GW + E]).then_inc(wh_ready, 1)
            act.wait_ge(loaded_k, 16)
            a_.copy(b2h[:], pk[:, K_B2:K_B2 + C]).then_inc(wh_ready, 1)
            a_.copy(sel_r[:], pk[:, K_SEL:K_SEL + JE * P]).then_inc(wh_ready, 1)

            def negate_m(g):
                act.wait_ge(tm_done, tm_at["m", g] + 1)
                rows = 2 * NS * TG * BT
                a_.mul(mneg[:, g, :], bank(5)[0:rows, 0:P], -1.0).then_inc(tm_read, 1)

            negate_m(0)
            for s in range(steps2):
                if s < T:
                    for hb in range(2):
                        u = 2 * s + hb
                        act.wait_ge(ST_done, u + 1)
                        if u == 0:
                            act.wait_ge(wl_ready, 3)
                        if s >= 2:
                            act.wait_ge(pl_ready, u - 3)
                        a_.activation(P32[:, s % 2, 512 * hb:512 * hb + 512], bank(2 + hb), ACT.Exp) \
                          .then_inc(exp_ready, 1)
                if ("m", (s + LEAD - 1) // TG) in tm_at and (s + LEAD - 1) % TG == TG - 1 \
                        and s + LEAD - 1 < T and (s + LEAD - 1) // TG > 0:
                    negate_m((s + LEAD - 1) // TG)
                i = s - 2
                if 0 <= i < T:
                    act.wait_ge(tm_done, tm_at["y", i] + 1)
                    if i >= 2:
                        act.wait_ge(wo_done, i - 1)
                    a_.copy(yT[:, i % 2], bank(5)[:, 0:P]).then_inc(tm_read, 1)
                i = s - 4
                if 0 <= i < T:
                    act.wait_ge(tm_done, tm_at["x", i] + 1)
                    if i >= 2:
                        act.wait_ge(x2l_ready, i - 1)
                    a_.copy(x2f[:, i % 2], bank(5)[:, 0:P]).then_inc(tm_read, 1)
                    act.wait_ge(tm_read, tm_at["x", i] + 1)
                    a_.copy(x2h[:, P * i:P * i + P], x2f[:, i % 2]).then_inc(x2h_ready, 1)
            act.wait_ge(gate_v, 2)
            a_.activation(gt[1][:], gt[0][:], ACT.Exp).then_inc(gate_e, 1)

            def silu(u):
                n, j = divmod(u, J)
                act.wait_ge(H1_done, u + 1)
                if u >= 2:
                    act.wait_ge(U_ready, u - 1)
                a_.activation(sil[:, u % 2], bank(u % 2), ACT.Silu, bias=pb[:, B_B1 + j:B_B1 + j + 1]) \
                  .then_inc(sil_ready, 1)

            def round_g(u):
                act.wait_ge(G_ready, u + 1)
                if u >= 3:
                    act.wait_ge(Y_part, u - 2)
                a_.copy(Gh[:, u % 3], G32[:, u % 2]).then_inc(gh_ready, 1)

            def copy_cT(n):
                act.wait_ge(cT_done, n + 1)
                a_.copy(cT[:, CH * n:CH * n + CH], bank(7)[0:2 * E, :]).then_inc(cT_ready, 1)

            def bias_y(n):
                act.wait_ge(Y_part, (n + 1) * J)
                if n >= 2:
                    act.wait_ge(oT_done, n - 1)
                a_.activation(yo[:, n % 2], bank(6), ACT.Identity, bias=pb[:, B_S2:B_S2 + 1]) \
                  .then_inc(yo_ready, 1)

            for u in range(UN + 3):
                if u < UN:
                    silu(u)
                if u == 1:
                    for n in range(NC):
                        copy_cT(n)
                if 1 <= u <= UN:
                    round_g(u - 1)
                if u >= J + 2 and (u - 2) % J == 0:
                    bias_y((u - 2) // J - 1)

        @block.vector
        def _(dve):
            v_ = nc.vector
            v_.memset(ex[:].rearrange("p s w -> p (s w)").bitcast(F32), 0.0).then_inc(ex_zero, 1)
            dve.wait_ge(ex_zero, 1)
            keys = ex[:].rearrange("p k (s h w) -> p k s h w", s=2, w=ROW)
            v_.memset(keys[:, :, 1, :, MROW], 1.0).then_inc(ex_zero, 1)

            def norm_stats(g):
                dve.wait_ge(loaded_x[g], 16)
                for t in range(g * TG, (g + 1) * TG):
                    v_.bn_stats(stat[:, t], xs[:, t]).then_inc(stats, 1)
                for t in range(g * TG, (g + 1) * TG):
                    dve.wait_ge(stats, t + 1)
                    v_.bn_aggr(mv[:, t], stat[:, t]).then_inc(mv_ready, 1)
                dve.wait_ge(mv_ready, (g + 1) * TG)
                v = mv[:, g * TG:(g + 1) * TG, 1]
                v_.tensor_scalar(v, v, EPS, None, ALU.add).then_inc(aggrs, TG)

            norm_stats(0)
            v_.memset(QM[:, 0].rearrange("p m h q -> p (m h q)").bitcast(F32), 0.0).then_inc(qm_zero, 1)
            for s in range(T + 3):
                if s < T:
                    if s % TG == 0:
                        dve.wait_ge(rstds, s // TG + 1)
                    if s >= 2:
                        dve.wait_ge(T_done, s - 1)
                    v_.tensor_scalar(xh[:, s % 2], xs[:, s], mv[:, s, 0:1], rstd[:, s:s + 1],
                                     ALU.subtract, ALU.mult).then_inc(xh_ready, 1)
                if s % TG == 0 and s // TG + 1 < G:
                    norm_stats(s // TG + 1)
                i = s - 1
                if 0 <= i < T:
                    dve.wait_ge(qkv_done, i + 1)
                    if i >= 2:
                        dve.wait_ge(rs_ready, i - 1)
                    if i == 0:
                        dve.wait_ge(loaded_a, 16)
                    qk = bank(2 + i % 2)[:, 0:2 * C]
                    v_.tensor_tensor(rt[:, i % 2, 0], qk, cos, ALU.mult).then_inc(rot_done, 1)
                    swapped = qk.rearrange("p (m w) -> p m w", w=2)[:, :, ::-1]
                    v_.tensor_tensor(rt[:, i % 2, 1].rearrange("p (m w) -> p m w", w=2), swapped,
                                     sin.rearrange("p (m w) -> p m w", w=2), ALU.mult).then_inc(rot_done, 1)
                    dve.wait_ge(vh_ready, BT * (i + 1))
                    for b in range(BT):
                        rows = slice(S * b, S * b + S)
                        src = bank(6 + i % 2)[rows, 0:C].rearrange("p (n h w) -> p n h w", h=2, w=D)
                        hi = Vh[rows, i].rearrange("p n (b h w) -> p n b h w", b=BT, w=VW)
                        lo = Vl[rows, i].rearrange("p n (b h w) -> p n b h w", b=BT, w=VW)
                        v_.tensor_tensor(lo[:, :, b, :, 0:D], src, hi[:, :, b, :, 0:D], ALU.subtract) \
                          .then_inc(vl_ready, 1)
                i = s - 3
                if 0 <= i < T:
                    dve.wait_ge(stackT_done, i + 1)
                    v_.tensor_copy(stk[:, :, i // TG, :, P * (i % TG):P * (i % TG) + P],
                                   bank(4 + i % 2).bitcast(F16).rearrange("p (k s m) -> p k s m", k=2, s=NS)) \
                      .then_inc(stk_ready, 1)

            def find_max(t):
                g, tl = divmod(t, TG)
                for b in range(BT):
                    dve.wait_ge(S_done, BT * t + b + 1)
                    dst = mx[:, g].rearrange("p (r s m) -> p s r m", r=2, s=NS)[:, :, :, tl * BT + b]
                    v_.tensor_reduce(dst, bank(b).rearrange("p (s r k) -> p s r k", s=NS, r=2), X, ALU.max) \
                      .then_inc(mx_ready, 1)

            for t in range(LEAD):
                find_max(t)
            for s in range(steps2):
                if s < T:
                    for hb in range(2):
                        u = 2 * s + hb
                        dve.wait_ge(exp_ready, u + 1)
                        if s >= 2:
                            dve.wait_ge(pv_done, s - 1)
                            dve.wait_ge(pl_ready, u - 3)
                        c = slice(512 * hb, 512 * hb + 512)
                        v_.tensor_copy(Ph[:, s % 2, c], P32[:, s % 2, c]).then_inc(ph_ready, 1)
                if max_tile(s) is not None:
                    find_max(max_tile(s))
                i = s - 1
                if 0 <= i < T:
                    dve.wait_ge(pv_done, i + 1)
                    o = bank(4)[:, 0:NP * VB].rearrange("p (n b h w) -> p n b h w", b=BT, h=2, w=VW)
                    v_.reciprocal(rsum[:, i % 2].rearrange("p (n b) -> p n b", b=BT), o[:, :, :, 0, D]) \
                      .then_inc(rsum_ready, 1)
                    dve.wait_ge(rsum_ready, i + 1)
                    if i >= 2:
                        dve.wait_ge(tm_done, tm_at["y", i - 2] + 1)
                    for h2 in range(2):
                        for b in range(BT):
                            rows = slice(S * h2, S * h2 + S)
                            rr = rsum[rows, i % 2].rearrange("p (n b) -> p n b", b=BT)[:, :, b]
                            dst = yt[S * b:S * b + S, i % 2].rearrange("p (n h w) -> p n h w", h=2, w=D)
                            v_.tensor_tensor(dst[:, :, h2], o[rows, :, b, h2, 0:D],
                                             rr.unsqueeze(2).broadcast_to([S, NP, D]), ALU.mult) \
                              .then_inc(yt_ready, 1)
                i = s - 3
                if 0 <= i < T:
                    dve.wait_ge(wo_done, i + 1)
                    v_.tensor_tensor(xs[:, i], bank(6)[:, 0:C], xs[:, i], ALU.add).then_inc(x1_ready, 1)
                    dve.wait_ge(x1_ready, i + 1)
                    v_.bn_stats(stat2[:, i], xs[:, i]).then_inc(st2, 1)
                    dve.wait_ge(st2, 2 * i + 1)
                    v_.bn_aggr(mv2[:, i], stat2[:, i]).then_inc(st2, 1)
                    dve.wait_ge(st2, 2 * i + 2)
                    v_.tensor_scalar(mv2[:, i, 1:2], mv2[:, i, 1:2], EPS, None, ALU.add).then_inc(ag2, 1)
                    dve.wait_ge(rstd2_ready, i + 1)
                    if i >= 2:
                        dve.wait_ge(tm_done, tm_at["x", i - 2] + 1)
                    v_.tensor_scalar(x2n[:, i % 2], xs[:, i], mv2[:, i, 0:1], rstd2[:, i:i + 1],
                                     ALU.subtract, ALU.mult).then_inc(x2n_ready, 1)

            steps = [0]

            def step(ins):
                steps[0] += 1
                ins.then_inc(gate_v, 1)
                dve.wait_ge(gate_v, steps[0])

            def over(a, shape, dim):
                return a.unsqueeze(dim).broadcast_to(shape)

            full = [P, T, E]
            lg = bank(7)[:, 0:T * E].rearrange("p (t e) -> p t e", e=E)
            dve.wait_ge(log_done, T)
            step(v_.tensor_reduce(tt[0][:], lg, X, ALU.max))
            step(v_.tensor_tensor(gt[0][:], lg, over(tt[0][:], full, 2), ALU.subtract))
            dve.wait_ge(gate_e, 1)
            step(v_.tensor_reduce(tt[1][:], gt[1][:], X, ALU.add))
            step(v_.reciprocal(tt[2][:], tt[1][:]))
            prob = gt[2][:]
            step(v_.tensor_tensor(prob, gt[1][:], over(tt[2][:], full, 2), ALU.mult))
            score = gt[3][:]
            step(v_.tensor_tensor(score, prob, over(gb, full, 1), ALU.add))
            two = score.rearrange("p t (g k w) -> p (t g) k w", g=NG, w=2)
            step(v_.tensor_tensor(pair[0][:], two[:, :, :, 0], two[:, :, :, 1], ALU.max))
            step(v_.tensor_tensor(pair[1][:], two[:, :, :, 0], two[:, :, :, 1], ALU.min))
            step(v_.tensor_tensor(gs[0][:], pair[0][:, :, 0], pair[0][:, :, 1], ALU.max))
            step(v_.tensor_tensor(gs[1][:], pair[0][:, :, 0], pair[0][:, :, 1], ALU.min))
            step(v_.tensor_tensor(gs[2][:], pair[1][:, :, 0], pair[1][:, :, 1], ALU.max))
            step(v_.tensor_tensor(gs[3][:], gs[1][:], gs[2][:], ALU.max))
            step(v_.tensor_tensor(gs[4][:], gs[0][:], gs[3][:], ALU.add))
            g4 = gs[4][:].rearrange("p (t g) -> p t g", g=NG)
            sq = [P, T, NG, NG]
            other, own = over(g4, sq, 2), over(g4, sq, 3)
            gtv = [gt[n][:].rearrange("p t (a b) -> p t a b", b=NG) for n in (4, 5, 6)]
            step(v_.tensor_tensor(gtv[0], other, own, ALU.is_gt))
            step(v_.tensor_tensor(gtv[1], other, own, ALU.is_equal))
            step(v_.tensor_tensor(gt[6][:], gt[5][:], over(below, full, 1), ALU.mult))
            step(v_.tensor_tensor(gt[5][:], gt[4][:], gt[6][:], ALU.add))
            step(v_.tensor_reduce(gs[5][:].rearrange("p (t g) -> p t g", g=NG), gtv[1], X, ALU.add))
            step(v_.tensor_scalar(gs[0][:], gs[5][:], 1.5, -BIG, ALU.is_gt, ALU.mult))
            kept = gt[4][:]
            step(v_.tensor_tensor(kept.rearrange("p t (g k) -> p t g k", k=GE),
                                  score.rearrange("p t (g k) -> p t g k", k=GE),
                                  over(gs[0][:].rearrange("p (t g) -> p t g", g=NG), [P, T, NG, GE], 3), ALU.add))

            def largest(src, sel, a, b, m1, m2):
                step(v_.tensor_reduce(m1, src, X, ALU.max))
                step(v_.tensor_tensor(a, src, over(m1, full, 2), ALU.is_equal))
                step(v_.tensor_tensor(b, a, over(rev, full, 1), ALU.mult))
                step(v_.tensor_reduce(m2, b, X, ALU.max))
                step(v_.tensor_tensor(sel, b, over(m2, full, 2), ALU.is_equal))

            largest(kept, gt[7][:], gt[5][:], gt[6][:], tt[3][:], tt[4][:])
            step(v_.scalar_tensor_tensor(out=gt[8][:], in0=gt[7][:], scalar=-BIGGER, in1=kept,
                                         op0=ALU.mult, op1=ALU.add))
            largest(gt[8][:], gt[9][:], gt[5][:], gt[6][:], tt[5][:], tt[6][:])
            step(v_.tensor_tensor(gt[5][:], gt[7][:], gt[9][:], ALU.add))
            step(v_.tensor_tensor(gt[6][:], gt[5][:], prob, ALU.mult))
            step(v_.tensor_copy(cc[:, :, 0:E], gt[6][:]))
            v_.tensor_tensor(cc[:, :, E:2 * E], gt[6][:], cc[:, :, 0:E].bitcast(F32), ALU.subtract) \
              .then_inc(cc_ready, 1)

            def gated(u):
                n, j = divmod(u, J)
                dve.wait_ge(H3_done, u + 1)
                dve.wait_ge(sil_ready, u + 1)
                if u >= 2:
                    dve.wait_ge(gl_ready, u - 1)
                shared = j == JE
                dst = G32 if shared else U
                ins = v_.scalar_tensor_tensor(out=dst[:, u % 2], in0=bank(2 + u % 2),
                                              scalar=pb[:, B_B3 + j:B_B3 + j + 1], in1=sil[:, u % 2],
                                              op0=ALU.add, op1=ALU.mult).then_inc(U_ready, 1)
                if shared:
                    dve.wait_ge(U_ready, u + 1)
                    v_.tensor_copy(tt[7][:, 0:1], G32[:, u % 2, 0:1]).then_inc(G_ready, 1)
                else:
                    dve.wait_ge(U_ready, u + 1)
                    dve.wait_ge(CR_done, n * JE + j + 1)
                    v_.tensor_tensor(G32[:, u % 2], bank(4 + (n * JE + j) % 2), U[:, u % 2], ALU.mult) \
                      .then_inc(G_ready, 1)

            def residual(n):
                dve.wait_ge(oT_done, n + 1)
                if n >= 2:
                    dve.wait_ge(stored[n % 2], 16 * (n // 2))
                v_.tensor_tensor(ob[:, n % 2], bank(7), xs[:, n * TG:(n + 1) * TG].rearrange("p t c -> p (t c)"),
                                 ALU.add).then_inc(ob_ready, 1)

            for u in range(UN + 4):
                if u < UN:
                    gated(u)
                if u >= J + 3 and (u - 3) % J == 0:
                    residual((u - 3) // J - 1)

        @block.tensor
        def _(pe):
            t_ = nc.tensor
            for s in range(T + 3):
                if s < T:
                    pe.wait_ge(xh_ready, s + 1)
                    if s == 0:
                        pe.wait_ge(loaded_a, 16)
                    if s % TG == 0:
                        pe.wait_ge(loaded_c[s // TG], 16)
                    if s >= 2:
                        pe.wait_ge(xcT_ready, s - 1)
                    t_.transpose(bank(s % 2)[:, 0:P], xh[:, s % 2], ident)
                    t_.transpose(bank(s % 2)[:, P:2 * P], cs[:, s % (CR * TG)], ident).then_inc(T_done, 1)
                i = s - 1
                if 0 <= i < T:
                    pe.wait_ge(xcT_ready, i + 1)
                    if i >= 2:
                        pe.wait_ge(rot_done, 2 * (i - 1))
                        pe.wait_ge(vl_ready, BT * (i - 1))
                    t_.matmul(bank(2 + i % 2)[:, 0:C], xcT[:, i % 2, 0:P], wq, start=True, stop=True)
                    t_.matmul(bank(2 + i % 2)[:, C:2 * C], xcT[:, i % 2, P:2 * P], wk, start=True, stop=True)
                    t_.matmul(bank(6 + i % 2)[:, 0:C], xcT[:, i % 2, P:2 * P], wv, start=True, stop=True) \
                      .then_inc(qkv_done, 1)
                i = s - 3
                if 0 <= i < T:
                    pe.wait_ge(lo_ready, 2 * (i + 1))
                    if i == 0:
                        pe.wait_ge(id16_ready, 1)
                    if i >= 2:
                        pe.wait_ge(stk_ready, i - 1)
                    for k in range(2 * NS):
                        last = t_.transpose(bank(4 + i % 2).bitcast(F16)[:, P * k:P * k + P],
                                            ex[:, i % 2, P * k:P * k + P], ident16[:])
                    last.then_inc(stackT_done, 1)

            def maxima(t):
                g, tl = divmod(t, TG)
                if tl == 0:
                    pe.wait_ge(qm_loaded[g], 16 * HQ)
                if t == 0:
                    pe.wait_ge(xcT_ready, T)
                for b in range(BT):
                    if t >= 1:
                        pe.wait_ge(mx_ready, BT * (t - 1) + b + 1)
                    m = tl * BT + b
                    for n in range(NP):
                        k, rh = divmod(n, 2)
                        two = QM[:, g % QR, k * TG * BT + m, 2 * rh:2 * rh + 2].rearrange("p h q -> p (h q)")
                        last = t_.matmul(bank(b)[:, S * n:S * n + S], two, stk[:, 1, g, k, S * m:S * m + S],
                                         start=True, stop=True)
                    last.then_inc(S_done, 1)

            def turn(use):
                n = tm_at[use]
                if n >= 1:
                    pe.wait_ge(tm_read, n)

            def turn_m(g):
                turn(("m", g))
                pe.wait_ge(mx_ready, BT * TG * (g + 1))
                if g == 0:
                    pe.wait_ge(stk_ready, T)
                t_.transpose(bank(5)[0:2 * NS * TG * BT, 0:P], mx[:, g], ident).then_inc(tm_done, 1)

            for t in range(TG):
                maxima(t)
            turn_m(0)
            for t in range(TG, LEAD):
                maxima(t)
            for s in range(steps2):
                if s < T:
                    g, tl = divmod(s, TG)
                    if tl == 0:
                        pe.wait_ge(m_moved[g], 16 * HQ)
                    if s == 0:
                        pe.wait_ge(rot_done, 2 * T)
                        pe.wait_ge(vl_ready, BT * T)
                    for hb in range(2):
                        if s >= 1:
                            pe.wait_ge(exp_ready, 2 * (s - 1) + hb + 1)
                        for k in (2 * hb, 2 * hb + 1):
                            for b in range(BT):
                                m = tl * BT + b
                                c = HQ * S * (k % 2)
                                last = t_.matmul(bank(2 + hb)[S * b:S * b + S, c:c + HQ * S],
                                                 stk[:, 1, g, k, S * m:S * m + S],
                                                 QM[:, g % QR, k * TG * BT + m].rearrange("p h q -> p (h q)"),
                                                 start=True, stop=True)
                        last.then_inc(ST_done, 1)
                if s + LEAD - 1 < T and (s + LEAD - 1) % TG == TG - 1 and (s + LEAD - 1) // TG > 0:
                    turn_m((s + LEAD - 1) // TG)
                if max_tile(s) is not None:
                    maxima(max_tile(s))
                i = s - 1
                if 0 <= i < T:
                    pe.wait_ge(pl_ready, 2 * (i + 1))
                    if i == 0:
                        pe.wait_ge(vl_ready, BT * T)
                    if i >= 1:
                        pe.wait_ge(yt_ready, 4 * i)
                    for n in range(NP):
                        o = bank(4)[:, VB * n:VB * n + VB]
                        c = slice(P * n, P * n + P)
                        t_.matmul(o, Ph[:, i % 2, c], Vh[:, i, n], start=True, stop=False)
                        t_.matmul(o, Ph[:, i % 2, c], Vl[:, i, n], start=False, stop=False)
                        last = t_.matmul(o, Pl[:, i % 2, c], Vh[:, i, n], start=False, stop=True)
                    last.then_inc(pv_done, 1)
                i = s - 2
                if 0 <= i < T:
                    turn(("y", i))
                    pe.wait_ge(yt_ready, 4 * (i + 1))
                    t_.transpose(bank(5)[:, 0:P], yt[:, i % 2], ident).then_inc(tm_done, 1)
                i = s - 3
                if 0 <= i < T:
                    pe.wait_ge(tm_read, tm_at["y", i] + 1)
                    if i == 0:
                        pe.wait_ge(loaded_b, 16)
                    if i >= 1:
                        pe.wait_ge(x1_ready, i)
                    t_.matmul(bank(6)[:, 0:C], yT[:, i % 2], wo, start=True, stop=True).then_inc(wo_done, 1)
                i = s - 4
                if 0 <= i < T:
                    turn(("x", i))
                    pe.wait_ge(x2n_ready, i + 1)
                    t_.transpose(bank(5)[:, 0:P], x2n[:, i % 2], ident).then_inc(tm_done, 1)
                i = s - 6
                if 0 <= i < T:
                    pe.wait_ge(x2l_ready, i + 1)
                    pe.wait_ge(wl_ready, 4)
                    c = slice(P * i, P * i + P)
                    o = bank(7)[:, E * i:E * i + E]
                    t_.matmul(o, x2h[:, c], gwh[:], start=True, stop=False)
                    t_.matmul(o, x2h[:, c], gwl[:], start=False, stop=False)
                    t_.matmul(o, x2l[:, c], gwh[:], start=False, stop=True).then_inc(log_done, 1)

            def split(o, n, j, mh, ml, start=True, stop=True):
                w = slice(P * j, P * j + P)
                t_.matmul(o, wh[n][:, w], mh, start=start, stop=False)
                t_.matmul(o, wh[n][:, w], ml, start=False, stop=False)
                return t_.matmul(o, wl[n][:, w], mh, start=False, stop=stop)

            def up(u):
                n, j = divmod(u, J)
                c = slice(CH * n, CH * n + CH)
                if u == 0:
                    pe.wait_ge(wl_ready, 5)
                    pe.wait_ge(mx_ready, BT * T)
                    pe.wait_ge(exp_ready, 2 * T)
                if u >= 2:
                    pe.wait_ge(sil_ready, u - 1)
                split(bank(u % 2), 0, j, x2h[:, c], x2l[:, c]).then_inc(H1_done, 1)
                if u >= 2:
                    pe.wait_ge(U_ready, u - 1)
                split(bank(2 + u % 2), 1, j, x2h[:, c], x2l[:, c]).then_inc(H3_done, 1)

            def spread(u):
                n, j = divmod(u, J)
                if j == JE:
                    return
                v = n * JE + j
                if j == 0:
                    pe.wait_ge(cT_ready, n + 1)
                if v >= 2:
                    pe.wait_ge(G_ready, (v - 2) // JE * J + (v - 2) % JE + 1)
                t_.matmul(bank(4 + v % 2), sel_r[:, P * j:P * j + P], cT[:, CH * n:CH * n + CH],
                          start=True, stop=True).then_inc(CR_done, 1)

            def down(u):
                n, j = divmod(u, J)
                pe.wait_ge(gl_ready, u + 1)
                if j == 0 and n >= 1:
                    pe.wait_ge(yo_ready, n)
                if j == 0:
                    c = slice(CH * n, CH * n + CH)
                    t_.matmul(bank(6), b2h[:], cT[:, c], start=True, stop=False)
                    t_.matmul(bank(6), b2l[:], cT[:, c], start=False, stop=False)
                split(bank(6), 2, j, Gh[:, u % 3], Gl[:, u % 3], start=False, stop=j == J - 1) \
                    .then_inc(Y_part, 1)

            def turn_out(n):
                pe.wait_ge(yo_ready, n + 1)
                if n == 0:
                    pe.wait_ge(cT_ready, NC)
                else:
                    pe.wait_ge(ob_ready, n)
                for t in range(TG):
                    last = t_.transpose(bank(7)[:, P * t:P * t + P], yo[:, n % 2, P * t:P * t + P], ident)
                last.then_inc(oT_done, 1)

            def turn_c(n):
                if n == 0:
                    pe.wait_ge(cc_ready, 1)
                else:
                    pe.wait_ge(cT_ready, n)
                for t in range(TG):
                    last = t_.transpose(bank(7)[0:2 * E, P * t:P * t + P],
                                        cc[:, n * TG + t].bitcast(F32), ident)
                last.then_inc(cT_done, 1)

            for u in range(UN + 4):
                if u < UN:
                    up(u)
                if u == 1:
                    for n in range(NC):
                        turn_c(n)
                    spread(0)
                if 1 <= u < UN:
                    spread(u)
                if 2 <= u < UN + 2:
                    down(u - 2)
                if u >= J + 3 and (u - 3) % J == 0:
                    turn_out((u - 3) // J - 1)


def kernel(x, ctx_1024, L0_xattn_Wq, L0_xattn_Wk, L0_xattn_Wv, L0_xattn_Wo, L0_ffn_gate_w, L0_ffn_gate_b,
           L0_ffn_We1, L0_ffn_be1, L0_ffn_We2, L0_ffn_be2, L0_ffn_We3, L0_ffn_be3, L0_ffn_ws1, L0_ffn_bs1,
           L0_ffn_ws2, L0_ffn_bs2, L0_ffn_ws3, L0_ffn_bs3):
    import numpy as np
    import concourse.bacc as bacc
    from concourse.bass_utils import run_bass_kernel_spmd

    f = lambda a: np.asarray(a)
    freqs = 1.0 / 10000.0 ** (np.arange(0, C, 2, dtype=np.float32) / C)
    ang = np.outer(np.arange(S, dtype=np.float32), freqs.astype(np.float32)).astype(np.float32)
    cosv = np.tile(np.repeat(np.cos(ang), 2, 1), (BT, 1))
    sinv = np.tile(np.repeat(np.sin(ang), 2, 1) * np.tile([-1.0, 1.0], C // 2), (BT, 1))
    scale = 1.0 / np.sqrt(D)
    cos = np.concatenate([cosv * scale, cosv], 1).astype(np.float32)
    sin = np.concatenate([sinv * scale, sinv], 1).astype(np.float32)
    ident = np.eye(P, dtype=np.float32)
    below = np.tile(np.tril(np.ones((NG, NG), np.float32), -1).reshape(1, -1), (P, 1))
    rev = np.tile(np.arange(E, 0, -1, dtype=np.float32), (P, 1))
    sel = (np.arange(2 * E)[:, None] % E == np.arange(E * I)[None, :] // I).astype(np.float32)

    col = lambda be, bs: np.concatenate([f(be).reshape(JE, P).T, f(bs).reshape(P, 1)], 1)
    pack_a = np.concatenate([f(L0_xattn_Wq).T, f(L0_xattn_Wk).T, f(L0_xattn_Wv).T, cos, sin, ident], 1)
    pack_b = np.concatenate([f(L0_xattn_Wo).T, f(L0_ffn_gate_w).T, np.tile(f(L0_ffn_gate_b).reshape(1, E), (P, 1)),
                             col(L0_ffn_be1, L0_ffn_bs1), col(L0_ffn_be3, L0_ffn_bs3),
                             f(L0_ffn_bs2).reshape(P, 1), below, rev], 1)
    pack_k = np.concatenate([np.tile(f(L0_ffn_be2), (2, 1)), sel], 1)
    up = lambda we, ws: np.concatenate([f(we).transpose(1, 0, 2).reshape(C, E * I), f(ws)], 1)
    w2 = np.concatenate([f(L0_ffn_We2).reshape(JE, P, C).transpose(1, 0, 2).reshape(P, JE * C), f(L0_ffn_ws2)], 1)
    arrays = {
        "in_x": f(x).reshape(TOK, C), "in_ctx": f(ctx_1024).reshape(TOK, C), "in_a": pack_a, "in_b": pack_b,
        "in_k": pack_k, "in_w1": up(L0_ffn_We1, L0_ffn_ws1), "in_w3": up(L0_ffn_We3, L0_ffn_ws3), "in_w2": w2,
    }
    arrays = {k: np.ascontiguousarray(v) for k, v in arrays.items()}
    nc = bacc.Bacc("TRN2", target_bir_lowering=False, num_devices=1)
    args = [nc.dram_tensor(k, v.shape, mybir.dt.from_np(v.dtype), kind="ExternalInput").ap()
            for k, v in arrays.items()]
    args.append(nc.dram_tensor("out", (TOK, C), F32, kind="ExternalOutput").ap())
    program(nc, *args)
    r = run_bass_kernel_spmd(nc, [arrays], core_ids=[0])
    return r.results[0]["out"].reshape(B, S, C)
```

```python
from contextlib import ExitStack

import concourse.bass as bass
from concourse import mybir

F32 = mybir.dt.float32
F32R = mybir.dt.float32r
F16 = mybir.dt.float16
ALU = mybir.AluOpType
ACT = mybir.ActivationFunctionType
X = mybir.AxisListType.X

P = 128
C = 128
B, S = 32, 64
H, D = 16, 8
E, I = 16, 64
NG, GE = 4, 4
TOK = B * S
T = TOK // P
BT = P // S
HQ = 4
NS = H // HQ
ROW = P // HQ
MROW = 3 * D
TG = 4
G = T // TG
NP = H // 2
VW = D + 1
VB = BT * 2 * VW
QR = 3
CH = 512
NC = TOK // CH
J = E * I // P + 1
JE = J - 1
CR = 2
EPS = 1e-5
BIG = 1e30
BIGGER = 1e32

ROUTE = [(0, 1), (1, 1), (2, 2)]
ROUTE_STEPS = 35
PARTS = 6
LO_SPLIT = 896
RT = TG * max(n for _, n in ROUTE)
RP = 3
RB = 3

A_WQ, A_WK, A_WV, A_COS, A_SIN, A_ID = 0, 128, 256, 384, 640, 896
A_N = 1024
B_WO, B_GW, B_GB, B_B1, B_B3, B_S2, B_LT, B_REV = 0, 128, 144, 160, 169, 178, 179, 195
B_N = 211
K_B2, K_SEL = 0, 128
K_N = 128 + JE * P


LAG = {
    "turn_out": 46, "maxima0": 16, "project_out": 27, "scores1": 23, "scores0": 23, "turn_y": 26, "up": 42,
    "maxima1": 16, "values": 25, "turn_x2": 29, "project": 2, "turn_tile": 1, "turn_stacks": 6,
    "turn_c": 38, "logits": 32, "turn_m": 16, "spread": 42, "down": 44,
    "store_yT": 26, "exp_logits": 33, "negate_m": 17, "store_stacks": 7, "exps1": 23, "exps0": 23,
    "hi_parts": 4, "store_x2": 29, "silu": 42, "store_cT": 38, "hi_g": 43, "store_turned": 1,
    "hi_probs": 23, "weights_hi": 7, "store_y": 44,
    "hi_values": 3, "lo_probs_d": 25, "route2": 34, "norm": 0, "rotate": 3, "add_attention": 27,
    "norm2": 28, "find_max": 16, "divide": 25, "read_logits": 32, "residual": 49, "zero_qm0": 0,
    "route0": 32, "nstats": 0, "route4": 35, "route3": 34, "route1": 33, "route5": 35, "lo_values": 3,
    "gated": 42,
    "lo_probs": 26, "weights_lo": 10, "lo_parts": 5, "zero_qm": 0, "lo_x2": 31, "deviation2": 28,
    "add_rotated": 3, "lo_g": 43, "dev": 0,
}

def program(nc, x, ctx_in, pack_a, pack_b, pack_k, w1, w3, w2, out):
    with ExitStack() as st:
        def sb(name, shape, dt=F32):
            return st.enter_context(nc.sbuf_tensor(name, shape, dt))

        def sem(name):
            return st.enter_context(nc.semaphore(name))

        xs = sb("xs", [P, T, C])
        pa = sb("pa", [P, A_N])
        pb = sb("pb", [P, B_N])
        sel_r = sb("sel_r", [2 * E, JE * P], F16)
        b2h = sb("b2h", [2 * E, C], F16)
        b2l = sb("b2l", [2 * E, C], F16)
        gwh = sb("gwh", [P, E], F32R)
        gwl = sb("gwl", [P, E], F32R)
        ident16 = sb("ident16", [P, P], F16)
        eps_t = sb("eps_t", [P, 1])
        stat = sb("stat", [P, T, 6])
        mv = sb("mv", [P, T, 2])
        rstd = sb("rstd", [P, T])
        stat2 = sb("stat2", [P, T, 6])
        mv2 = sb("mv2", [P, T, 2])
        rstd2 = sb("rstd2", [P, T])
        mhalf = sb("mhalf", [P, T])
        Vh = sb("Vh", [P, T, NP, VB], F16)
        Vl = sb("Vl", [P, T, NP, VB], F16)
        x2h = sb("x2h", [P, TOK], F32R)
        x2l = sb("x2l", [P, TOK], F32R)
        wh = [sb(f"w{n}h", [P, J * P], F32R) for n in (1, 3, 2)]
        wl = [sb(f"w{n}l", [P, J * P], F32R) for n in (1, 3, 2)]
        mx = sb("mx", [P, G, 2 * NS * TG * BT])
        mneg = sb("mneg", [2 * NS * TG * BT, 2, P], F16)
        rsum = sb("rsum", [P, RB, NP * BT])
        yt = sb("yt", [P, RB, C])
        yT = sb("yT", [P, RB, P])
        x2n = sb("x2n", [P, RB, C])
        x2f = sb("x2f", [P, RB, P])
        shared = sb("shared", [P, 3 * J * P + K_N])
        pk = shared[0:2 * E, 3 * J * P:3 * J * P + K_N]
        wraw = [shared[:, n * J * P:(n + 1) * J * P] for n in range(3)]
        P32 = shared[:, 0:2048].rearrange("p (s m) -> p s m", s=2)
        Ph = shared[:, 2048:2048 + 512 * RP].bitcast(F16).rearrange("p (s m) -> p s m", s=RP)
        Pl = shared[:, 2048 + 512 * RP:3072 + 512 * RP].bitcast(F16).rearrange("p (s m) -> p s m", s=2)
        stk = sb("stk", [P, G, NS, TG * P], F16)
        cT = sb("cT", [2 * E, TOK], F16)
        lgs = sb("lgs", [P, T, E])
        gt = [sb(f"gt{n}", [P, RT, E]) for n in range(7)]
        pair = [sb(f"pair{n}", [P, RT * NG, 2]) for n in range(2)]
        gs = [sb(f"gs{n}", [P, RT * NG]) for n in range(6)]
        tt = [sb(f"tt{n}", [P, RT]) for n in range(7)]
        hi16 = sb("hi16", [P, RT, E], F16)
        cc = sb("cc", [P, T, 2 * E])

        with ExitStack() as early:
            def eb(name, shape, dt=F32):
                return early.enter_context(nc.sbuf_tensor(name, shape, dt))

            cs = eb("cs", [P, CR * TG, C])
            xh = eb("xh", [P, 2, C])
            xcT = eb("xcT", [P, 2, 2 * P])
            rt = eb("rt", [P, 2, 2, 2 * C])
            rs = eb("rs", [P, 3, 2 * C])
            ex = eb("ex", [P, 3, 2 * NS * P], F16)
            stq = eb("stq", [P, 2, NS, TG * P], F16)
            QM = eb("QM", [P, QR, NS * TG * BT, HQ, S], F16)
        sil = sb("sil", [P, 2, CH])
        U = sb("U", [P, 2, CH])
        G32 = sb("G32", [P, 2, CH])
        Gh = sb("Gh", [P, 3, CH], F32R)
        Gl = sb("Gl", [P, 3, CH], F32R)
        yo = sb("yo", [P, 2, CH])
        ob = sb("ob", [P, 2, CH])

        ps = st.enter_context(nc.psum_tensor("ps", [P, 8, 512], F32))

        def bank(n):
            return ps[:, n, :]

        wq = pa[:, A_WQ:A_WQ + C]
        wkv = pa[:, A_WK:A_WK + 2 * C]
        cos = pa[:, A_COS:A_COS + 2 * C]
        sin = pa[:, A_SIN:A_SIN + 2 * C]
        ident = pa[:, A_ID:A_ID + P]
        wo = pb[:, B_WO:B_WO + C]
        gb = pb[:, B_GB:B_GB + E]
        below = pb[:, B_LT:B_LT + NG * NG]
        rev = pb[:, B_REV:B_REV + E]

        loaded_a = sem("loaded_a")
        loaded_b = sem("loaded_b")
        loaded_k = sem("loaded_k")
        loaded_x = [sem(f"loaded_x{g}") for g in range(G)]
        loaded_c = [sem(f"loaded_c{g}") for g in range(G)]
        loaded_w = [sem(f"loaded_w{n}") for n in range(3)]
        qm_loaded = [sem(f"qm_loaded{g}") for g in range(G)]
        m_moved = [sem(f"m_moved{g}") for g in range(G)]
        stored = [sem(f"stored{n}") for n in range(2)]
        qm_zero = sem("qm_zero")
        qm_zero0 = sem("qm_zero0")
        ex_zero = sem("ex_zero")
        vh_zero = sem("vh_zero")
        vl_zero = sem("vl_zero")
        consts = sem("consts")
        id16_ready = sem("id16_ready")
        stats = sem("stats")
        mv_ready = sem("mv_ready")
        aggrs = sem("aggrs")
        rstds = sem("rstds")
        xh_ready = sem("xh_ready")
        T_done = sem("T_done")
        xcT_ready = sem("xcT_ready")
        qkv_done = sem("qkv_done")
        rot_done = sem("rot_done")
        rs_ready = sem("rs_ready")
        hi_ready = sem("hi_ready")
        lo_ready = sem("lo_ready")
        vh_ready = sem("vh_ready")
        vl_ready = sem("vl_ready")
        stackT_done = sem("stackT_done")
        stk_ready = sem("stk_ready")
        wh_ready = sem("wh_ready")
        wl_ready = sem("wl_ready")
        S_done = [sem(f"S_done{n}") for n in range(2)]
        mx_ready = sem("mx_ready")
        mT_done = sem("mT_done")
        mT_read = sem("mT_read")
        ST_done = [sem(f"ST_done{n}") for n in range(2)]
        exp_ready = [sem(f"exp_ready{n}") for n in range(2)]
        ph_ready = sem("ph_ready")
        pl_ready = sem("pl_ready")
        pld_ready = sem("pld_ready")
        pv_done = sem("pv_done")
        rsum_ready = sem("rsum_ready")
        yt_ready = sem("yt_ready")
        yT_done = sem("yT_done")
        yT_ready = sem("yT_ready")
        wo_done = sem("wo_done")
        x1_ready = sem("x1_ready")
        st2 = sem("st2")
        ag2 = sem("ag2")
        rstd2_ready = sem("rstd2_ready")
        x2n_ready = sem("x2n_ready")
        xT_done = sem("xT_done")
        x2f_ready = sem("x2f_ready")
        x2h_ready = sem("x2h_ready")
        x2l_ready = sem("x2l_ready")
        log_done = sem("log_done")
        log_read = sem("log_read")
        routed = sem("routed")
        route_exp = sem("route_exp")
        cc_ready = sem("cc_ready")
        cT_done = sem("cT_done")
        cT_ready = sem("cT_ready")
        H1_done = sem("H1_done")
        H3_done = sem("H3_done")
        CR_done = sem("CR_done")
        sil_ready = sem("sil_ready")
        U_ready = sem("U_ready")
        G_ready = sem("G_ready")
        gh_ready = sem("gh_ready")
        gl_ready = sem("gl_ready")
        Y_part = sem("Y_part")
        yo_ready = sem("yo_ready")
        oT_done = sem("oT_done")
        ob_ready = sem("ob_ready")

        UN = NC * J
        STEPS = max(LAG[n] for n in ("turn_out", "residual", "store_y", "down", "lo_g", "hi_g")) + UN

        def met(s, what, count):
            i = s - LAG[what]
            return [i] if 0 <= i < count else []

        def tile_at(s, what):
            return met(s, what, T)

        def unit_at(s, what):
            return met(s, what, UN)

        def group_at(s, what):
            return [i // TG for i in met(s, what, T) if i % TG == TG - 1]

        def next_group_at(s, what):
            return [i // TG + 1 for i in met(s, what, T) if i % TG == 0 and i // TG + 1 < G]

        def chunk_at(s, what):
            return [i // J for i in met(s, what, UN) if i % J == J - 1]

        def round_at(s, what):
            return [r for i in met(s, what, T) for r, (g, n) in enumerate(ROUTE) if i == TG * (g + n) - 1]

        def routed_at(s, what):
            return [ROUTE[r][0] + k for r in round_at(s, what) for k in range(ROUTE[r][1])]

        def unit(u):
            n, jj = divmod(u, J)
            return n, (jj - 1) % J

        early_units = max(0, LAG["scores1"] + T - LAG["up"])

        def pair_of(u):
            if u < early_units:
                return 2, u - 1
            if (u - early_units) % 2 == 0:
                return 0, (u - 2 if u > early_units else -1)
            return 2, (u - 2 if u > early_units + 1 else early_units - 1)

        route_base = [ROUTE_STEPS * r for r in range(len(ROUTE))]

        own_w = min(T, max(0, LAG["up"] - LAG["project_out"]))
        own_x = min(T, max(0, LAG["up"] - LAG["turn_x2"]))

        def tiles_before(what, s, same):
            return max(0, min(T, s - LAG[what] + (1 if same else 0)))

        turns = []
        for s in range(STEPS):
            turns += [("o", n) for n in chunk_at(s, "turn_out")]
            turns += [("w", i) for i in tile_at(s, "project_out") if i >= own_w]
            turns += [("y", i) for i in tile_at(s, "turn_y")]
            turns += [("x", i) for i in tile_at(s, "turn_x2") if i >= own_x]
            turns += [("c", n) for n in routed_at(s, "turn_c")]

        def since(use):
            n = turns.index(use)
            if n == 0:
                return stk_ready, T
            what, k = turns[n - 1]
            return {"w": (x1_ready, k + 1), "y": (yT_ready, k + 1), "x": (x2f_ready, k + 1),
                    "c": (cT_ready, k + 1), "o": (ob_ready, k + 1)}[what]

        LG = NP * VB

        x_v = x.rearrange("(g t p) c -> g p t c", g=G, p=P)
        c_v = ctx_in.rearrange("(g t p) c -> g p t c", g=G, p=P)
        o_v = out.rearrange("(n t p) c -> n p t c", n=NC, p=P)

        block = st.enter_context(nc.Block())

        @block.sync
        def _(sp):
            sp.dma_start(xs[:, 0:TG, :], x_v[0]).then_inc(loaded_x[0], 16)
            sp.dma_start(pa[:], pack_a).then_inc(loaded_a, 16)
            sp.dma_start(cs[:, 0:TG, :], c_v[0]).then_inc(loaded_c[0], 16)
            for g in range(1, G):
                sp.dma_start(xs[:, g * TG:(g + 1) * TG, :], x_v[g]).then_inc(loaded_x[g], 16)
                if g < CR:
                    sp.dma_start(cs[:, g * TG:(g + 1) * TG, :], c_v[g]).then_inc(loaded_c[g], 16)
            sp.dma_start(pb[:], pack_b).then_inc(loaded_b, 16)
            for n, w in enumerate((w1, w3, w2)):
                sp.dma_start(wraw[n], w).then_inc(loaded_w[n], 16)
            sp.dma_start(pk, pack_k).then_inc(loaded_k, 16)

            def load_c(g):
                sp.wait_ge(T_done, (g - CR + 1) * TG)
                slot = g % CR * TG
                sp.dma_start(cs[:, slot:slot + TG, :], c_v[g]).then_inc(loaded_c[g], 16)

            def load_qm(g):
                sp.wait_ge(stk_ready, (g + 1) * TG)
                sp.wait_ge(qm_zero0, 4)
                if g >= 1:
                    sp.wait_ge(qm_zero, 4 * min(g, QR - 1))
                if g >= QR:
                    for hb in range(2):
                        sp.wait_ge(ST_done[hb], TG * (g - QR + 1))
                for r in range(HQ):
                    rows = slice(ROW * r, ROW * r + ROW)
                    sp.dma_start(QM[rows, g % QR, :, r, :],
                                 stq[rows, g % 2].rearrange("p s (m q) -> p (s m) q", q=S)) \
                        .then_inc(qm_loaded[g], 16)

            def move_m(g):
                sp.wait_ge(mT_read, g + 1)
                half = NS * TG * BT
                for r in range(HQ):
                    rh, r2 = divmod(r, 2)
                    row = ROW * r + MROW
                    sp.dma_start(QM[row:row + 1, g % QR, :, r, :],
                                 mneg[half * rh:half * rh + half, g % 2, S * r2:S * r2 + S]) \
                        .then_inc(m_moved[g], 16)

            load_c(2)
            load_c(3)
            for g in range(QR):
                load_qm(g)
            move_m(0)
            move_m(1)
            for g in range(QR, G):
                load_qm(g)
                move_m(g - 1)
            move_m(G - 1)
            for n in range(NC):
                sp.wait_ge(ob_ready, n + 1)
                sp.dma_start(o_v[n], ob[:, n % 2, :].rearrange("p (t c) -> p t c", c=C)) \
                    .then_inc(stored[n % 2], 16)
            for n in range(2):
                sp.wait_ge(stored[n], 16 * (NC // 2))

        @block.gpsimd
        def _(pool):
            g_ = nc.gpsimd
            g_.memset(mhalf[:], -0.5).then_inc(consts, 1)

            def deviations(g):
                pool.wait_ge(consts, 1)
                pool.wait_ge(aggrs, (g + 1) * TG)
                c = slice(g * TG, (g + 1) * TG)
                g_.tensor_tensor(rstd[:, c], mv[:, c, 1], mhalf[:, 0:TG], ALU.pow).then_inc(rstds, 1)

            def add_rotated(i):
                pool.wait_ge(rot_done, 2 * (i + 1))
                if i >= 3:
                    pool.wait_ge(lo_ready, 2 * (i - 2))
                g_.tensor_tensor(rs[:, i % 3], rt[:, i % 2, 0], rt[:, i % 2, 1], ALU.add).then_inc(rs_ready, 1)

            def lo_parts(i):
                pool.wait_ge(hi_ready, i + 1)
                pool.wait_ge(rs_ready, i + 1)
                o = ex[:, i % 3].rearrange("p (s h w) -> p s h w", s=2, w=ROW)
                src = rs[:, i % 3].rearrange("p (s h w) -> p s h w", s=2, w=D)
                g_.tensor_tensor(o[:, 0, :, 0:D], src[:, 0], o[:, 0, :, D:2 * D], ALU.subtract) \
                  .then_inc(lo_ready, 1)
                g_.tensor_tensor(o[:, 1, :, 2 * D:3 * D], src[:, 1], o[:, 1, :, D:2 * D], ALU.subtract) \
                  .then_inc(lo_ready, 1)

            def weight_lo(n):
                pool.wait_ge(wh_ready, n + 1)
                g_.tensor_tensor(wl[n][:], wraw[n], wh[n][:].bitcast(F32), ALU.subtract).then_inc(wl_ready, 1)

            def zero_qm(i):
                if 0 <= i < 4 * (QR - 1):
                    q, k = 1 + i // 4, slice(TG * NS * BT // 4 * (i % 4), TG * NS * BT // 4 * (i % 4 + 1))
                    g_.memset(QM[:, q, k].rearrange("p m h q -> p (m h q)").bitcast(F32), 0.0).then_inc(qm_zero, 1)

            deviations(0)
            for b in range(BT):
                if b == 0:
                    pool.wait_ge(vh_zero, 1)
                else:
                    pool.wait_ge(vh_zero, 1 + b)
                ones = Vh[S * b:S * b + S].rearrange("p t n (b h w) -> p (t n) b h w", b=BT, w=VW)
                g_.memset(ones[:, :, b, :, D], 1.0).then_inc(vh_zero, 1)
            pool.wait_ge(vh_zero, 1 + BT)
            def weights(i):
                if i >= 0 and i % 3 == 0 and i < 9:
                    weight_lo(i // 3)
                if i == 9:
                    pool.wait_ge(wh_ready, 5)
                    g_.tensor_tensor(gwl[:], pb[:, B_GW:B_GW + E], gwh[:].bitcast(F32), ALU.subtract).then_inc(wl_ready, 1)
                    g_.tensor_tensor(b2l[:], pk[:, K_B2:K_B2 + C], b2h[:], ALU.subtract).then_inc(wl_ready, 1)

            def lo_probs(i):
                pool.wait_ge(ph_ready, i + 1)
                if i >= 2:
                    pool.wait_ge(pv_done, i - 1)
                g_.tensor_tensor(Pl[:, i % 2, 0:LO_SPLIT], P32[:, i % 2, 0:LO_SPLIT], Ph[:, i % RP, 0:LO_SPLIT],
                                 ALU.subtract).then_inc(pl_ready, 1)

            def deviation2(i):
                pool.wait_ge(ag2, i + 1)
                g_.tensor_tensor(rstd2[:, i:i + 1], mv2[:, i, 1:2], mhalf[:, 0:1], ALU.pow) \
                  .then_inc(rstd2_ready, 1)

            def lo_x2(i):
                pool.wait_ge(x2h_ready, i + 1)
                c = slice(P * i, P * i + P)
                g_.tensor_tensor(x2l[:, c], x2f[:, i % RB], x2h[:, c].bitcast(F32), ALU.subtract) \
                  .then_inc(x2l_ready, 1)

            def lo_g(u):
                pool.wait_ge(gh_ready, u + 1)
                if u >= 3:
                    pool.wait_ge(Y_part, u - 2)
                g_.tensor_tensor(Gl[:, u % 3], G32[:, u % 2], Gh[:, u % 3].bitcast(F32), ALU.subtract) \
                  .then_inc(gl_ready, 1)

            for s in range(STEPS):
                for i in tile_at(s, "lo_probs"):
                    lo_probs(i)
                for i in tile_at(s, "weights_lo"):
                    weights(i)
                for i in tile_at(s, "lo_parts"):
                    lo_parts(i)
                for i in tile_at(s, "zero_qm"):
                    zero_qm(i)
                for i in tile_at(s, "lo_x2"):
                    lo_x2(i)
                for i in tile_at(s, "deviation2"):
                    deviation2(i)
                for i in tile_at(s, "add_rotated"):
                    add_rotated(i)
                for u in unit_at(s, "lo_g"):
                    lo_g(u)
                for g in next_group_at(s, "dev"):
                    deviations(g)

        @block.scalar
        def _(act):
            a_ = nc.scalar
            a_.memzero(Vh[:].rearrange("p t n w -> p (t n w)")).then_inc(vh_zero, 1)
            a_.memzero(Vl[:].rearrange("p t n w -> p (t n w)")).then_inc(vl_zero, 1)
            act.wait_ge(loaded_a, 16)
            a_.copy(ident16[:], ident).then_inc(id16_ready, 1)

            def store_stacks(i):
                act.wait_ge(stackT_done, i + 1)
                g, c = i // TG, slice(P * (i % TG), P * (i % TG) + P)
                src = bank(4 + i % 2).bitcast(F16).rearrange("p (k s m) -> p k s m", k=2, s=NS)
                if i % TG == 0 and g >= 2:
                    act.wait_ge(qm_loaded[g - 2], 16 * HQ)
                a_.copy(stq[:, g % 2, :, c], src[:, 0])
                a_.copy(stk[:, g, :, c], src[:, 1]).then_inc(stk_ready, 1)

            def store_turned(i):
                act.wait_ge(T_done, i + 1)
                if i >= 2:
                    act.wait_ge(qkv_done, i - 1)
                a_.copy(xcT[:, i % 2], bank(i % 2)[:, 0:2 * P]).then_inc(xcT_ready, 1)

            def hi_parts(i):
                act.wait_ge(rs_ready, i + 1)
                if i == 0:
                    act.wait_ge(ex_zero, 2)
                if i >= 3:
                    act.wait_ge(stackT_done, i - 2)
                o = ex[:, i % 3].rearrange("p (s h w) -> p s h w", s=2, w=ROW)
                src = rs[:, i % 3].rearrange("p (s h w) -> p s h w", s=2, w=D)
                for side, first in ((0, D), (1, 0)):
                    dst = o[:, side, :, first:first + 2 * D].rearrange("p h (k w) -> p h k w", k=2)
                    last = a_.copy(dst, src[:, side].unsqueeze(2).broadcast_to([P, H, 2, D]))
                last.then_inc(hi_ready, 1)

            def weight_hi(n):
                act.wait_ge(loaded_w[n], 16)
                a_.copy(wh[n][:], wraw[n]).then_inc(wh_ready, 1)

            def negate_m(g):
                act.wait_ge(mT_done, g + 1)
                if g >= 2:
                    act.wait_ge(m_moved[g - 2], 16 * HQ)
                rows = 2 * NS * TG * BT
                a_.mul(mneg[:, g % 2, :], bank(7)[0:rows, 0:P], -1.0).then_inc(mT_read, 1)

            def weights(i):
                if i >= 0 and i % 3 == 0 and i < 9:
                    weight_hi(i // 3)
                if i == 9:
                    act.wait_ge(loaded_b, 16)
                    a_.copy(gwh[:], pb[:, B_GW:B_GW + E]).then_inc(wh_ready, 1)
                    act.wait_ge(loaded_k, 16)
                    a_.copy(b2h[:], pk[:, K_B2:K_B2 + C]).then_inc(wh_ready, 1)
                    a_.copy(sel_r[:], pk[:, K_SEL:K_SEL + JE * P]).then_inc(wh_ready, 1)

            def exps(i, hb):
                act.wait_ge(ST_done[hb], i + 1)
                if i == 0:
                    act.wait_ge(wl_ready, 5)
                if i >= 2:
                    act.wait_ge(pl_ready, i - 1)
                    act.wait_ge(pld_ready, i - 1)
                a_.activation(P32[:, i % 2, 512 * hb:512 * hb + 512], bank(hb), ACT.Exp).then_inc(exp_ready[hb], 1)

            def hi_probs(i):
                for hb in range(2):
                    act.wait_ge(exp_ready[hb], i + 1)
                if i >= RP:
                    act.wait_ge(pv_done, i - RP + 1)
                a_.copy(Ph[:, i % RP], P32[:, i % 2]).then_inc(ph_ready, 1)

            def store_yT(i):
                act.wait_ge(yT_done, i + 1)
                if i >= RB:
                    act.wait_ge(wo_done, i - RB + 1)
                a_.copy(yT[:, i % RB], bank(5)[:, 0:P]).then_inc(yT_ready, 1)

            def store_x2(i):
                act.wait_ge(xT_done, i + 1)
                if i >= RB:
                    act.wait_ge(x2l_ready, i - RB + 1)
                a_.copy(x2f[:, i % RB], bank(3 if i < own_x else 5)[:, 0:P]).then_inc(x2f_ready, 1)
                act.wait_ge(x2f_ready, i + 1)
                a_.copy(x2h[:, P * i:P * i + P], x2f[:, i % RB]).then_inc(x2h_ready, 1)

            def exp_logits(r):
                act.wait_ge(routed, route_base[r] + 2)
                n = TG * ROUTE[r][1]
                a_.activation(gt[1][:, 0:n], gt[0][:, 0:n], ACT.Exp).then_inc(route_exp, 1)

            def silu(u):
                n, j = unit(u)
                act.wait_ge(H1_done, u + 1)
                if u >= 2:
                    act.wait_ge(U_ready, u - 1)
                a_.activation(sil[:, u % 2], bank(pair_of(u)[0]), ACT.Silu, bias=pb[:, B_B1 + j:B_B1 + j + 1]) \
                  .then_inc(sil_ready, 1)

            def hi_g(u):
                n, j = unit(u)
                if j == JE:
                    act.wait_ge(U_ready, u + 1)
                else:
                    act.wait_ge(G_ready, n * JE + j + 1)
                if u >= 3:
                    act.wait_ge(Y_part, u - 2)
                a_.copy(Gh[:, u % 3], G32[:, u % 2]).then_inc(gh_ready, 1)

            def store_cT(n):
                act.wait_ge(cT_done, n + 1)
                a_.copy(cT[:, CH * n:CH * n + CH], bank(5)[0:2 * E, :]).then_inc(cT_ready, 1)

            def store_y(n):
                act.wait_ge(Y_part, (n + 1) * J)
                if n >= 2:
                    act.wait_ge(oT_done, n - 1)
                a_.activation(yo[:, n % 2], bank(6), ACT.Identity, bias=pb[:, B_S2:B_S2 + 1]) \
                  .then_inc(yo_ready, 1)

            for s in range(STEPS):
                for i in tile_at(s, "store_yT"):
                    store_yT(i)
                for r in round_at(s, "exp_logits"):
                    exp_logits(r)
                for g in group_at(s, "negate_m"):
                    negate_m(g)
                for i in tile_at(s, "store_stacks"):
                    store_stacks(i)
                for i in tile_at(s, "exps1"):
                    exps(i, 1)
                for i in tile_at(s, "exps0"):
                    exps(i, 0)
                for i in tile_at(s, "hi_parts"):
                    hi_parts(i)
                for i in tile_at(s, "store_x2"):
                    store_x2(i)
                for u in unit_at(s, "silu"):
                    silu(u)
                for n in routed_at(s, "store_cT"):
                    store_cT(n)
                for u in unit_at(s, "hi_g"):
                    hi_g(u)
                for i in tile_at(s, "store_turned"):
                    store_turned(i)
                for i in tile_at(s, "hi_probs"):
                    hi_probs(i)
                for i in tile_at(s, "weights_hi"):
                    weights(i)
                for n in chunk_at(s, "store_y"):
                    store_y(n)

        @block.vector
        def _(dve):
            v_ = nc.vector
            v_.memset(ex[:].rearrange("p s w -> p (s w)").bitcast(F32), 0.0).then_inc(ex_zero, 1)
            dve.wait_ge(ex_zero, 1)
            keys = ex[:].rearrange("p k (s h w) -> p k s h w", s=2, w=ROW)
            v_.memset(keys[:, :, 1, :, MROW], 1.0).then_inc(ex_zero, 1)

            def norm_stats(g):
                dve.wait_ge(loaded_x[g], 16)
                for t in range(g * TG, (g + 1) * TG):
                    v_.bn_stats(stat[:, t], xs[:, t]).then_inc(stats, 1)
                for t in range(g * TG, (g + 1) * TG):
                    dve.wait_ge(stats, t + 1)
                    v_.bn_aggr(mv[:, t], stat[:, t]).then_inc(mv_ready, 1)
                dve.wait_ge(mv_ready, (g + 1) * TG)
                v = mv[:, g * TG:(g + 1) * TG, 1]
                v_.tensor_scalar(v, v, EPS, None, ALU.add).then_inc(aggrs, TG)

            def norm(i):
                dve.wait_ge(rstds, i // TG + 1)
                if i >= 2:
                    dve.wait_ge(T_done, i - 1)
                v_.tensor_scalar(xh[:, i % 2], xs[:, i], mv[:, i, 0:1], rstd[:, i:i + 1],
                                 ALU.subtract, ALU.mult).then_inc(xh_ready, 1)

            def rotate(i):
                dve.wait_ge(qkv_done, i + 1)
                if i >= 2:
                    dve.wait_ge(rs_ready, i - 1)
                if i == 0:
                    dve.wait_ge(loaded_a, 16)
                qk = bank(2 + i % 2)[:, 0:2 * C]
                v_.tensor_tensor(rt[:, i % 2, 0], qk, cos, ALU.mult).then_inc(rot_done, 1)
                swapped = qk.rearrange("p (m w) -> p m w", w=2)[:, :, ::-1]
                v_.tensor_tensor(rt[:, i % 2, 1].rearrange("p (m w) -> p m w", w=2), swapped,
                                 sin.rearrange("p (m w) -> p m w", w=2), ALU.mult).then_inc(rot_done, 1)

            def hi_values(i):
                dve.wait_ge(qkv_done, i + 1)
                if i == 0:
                    dve.wait_ge(vh_zero, 1 + BT)
                for b in range(BT):
                    rows = slice(S * b, S * b + S)
                    src = bank(2 + i % 2)[rows, 2 * C:3 * C].rearrange("p (n h w) -> p n h w", h=2, w=D)
                    dst = Vh[rows, i].rearrange("p n (b h w) -> p n b h w", b=BT, w=VW)
                    v_.tensor_copy(dst[:, :, b, :, 0:D], src).then_inc(vh_ready, 1)

            def lo_values(i):
                dve.wait_ge(vh_ready, BT * (i + 1))
                if i == 0:
                    dve.wait_ge(vl_zero, 1)
                for b in range(BT):
                    rows = slice(S * b, S * b + S)
                    src = bank(2 + i % 2)[rows, 2 * C:3 * C].rearrange("p (n h w) -> p n h w", h=2, w=D)
                    hi = Vh[rows, i].rearrange("p n (b h w) -> p n b h w", b=BT, w=VW)
                    lo = Vl[rows, i].rearrange("p n (b h w) -> p n b h w", b=BT, w=VW)
                    v_.tensor_tensor(lo[:, :, b, :, 0:D], src, hi[:, :, b, :, 0:D], ALU.subtract) \
                      .then_inc(vl_ready, 1)

            def find_max(t):
                g, tl = divmod(t, TG)
                for b in range(BT):
                    dve.wait_ge(S_done[b], t + 1)
                    dst = mx[:, g].rearrange("p (r s m) -> p s r m", r=2, s=NS)[:, :, :, tl * BT + b]
                    v_.tensor_reduce(dst, bank(6 + b).rearrange("p (s r k) -> p s r k", s=NS, r=2), X, ALU.max) \
                      .then_inc(mx_ready, 1)

            def zero_qm(i):
                if 0 <= i < 4:
                    k = slice(TG * NS * BT // 4 * (i % 4), TG * NS * BT // 4 * (i % 4 + 1))
                    v_.memset(QM[:, 0, k].rearrange("p m h q -> p (m h q)").bitcast(F32), 0.0).then_inc(qm_zero0, 1)

            norm_stats(0)
            def lo_probs(i):
                dve.wait_ge(ph_ready, i + 1)
                if i >= 2:
                    dve.wait_ge(pv_done, i - 1)
                a, b = LO_SPLIT, 1024
                v_.tensor_tensor(Pl[:, i % 2, a:b], P32[:, i % 2, a:b], Ph[:, i % RP, a:b], ALU.subtract) \
                  .then_inc(pld_ready, 1)

            def divide(i):
                dve.wait_ge(pv_done, i + 1)
                o = bank(4)[:, 0:NP * VB].rearrange("p (n b h w) -> p n b h w", b=BT, h=2, w=VW)
                v_.reciprocal(rsum[:, i % RB].rearrange("p (n b) -> p n b", b=BT), o[:, :, :, 0, D]) \
                  .then_inc(rsum_ready, 1)
                dve.wait_ge(rsum_ready, i + 1)
                if i >= RB:
                    dve.wait_ge(yT_done, i - RB + 1)
                for h2 in range(2):
                    for b in range(BT):
                        rows = slice(S * h2, S * h2 + S)
                        rr = rsum[rows, i % RB].rearrange("p (n b) -> p n b", b=BT)[:, :, b]
                        dst = yt[S * b:S * b + S, i % RB].rearrange("p (n h w) -> p n h w", h=2, w=D)
                        v_.tensor_tensor(dst[:, :, h2], o[rows, :, b, h2, 0:D],
                                         rr.unsqueeze(2).broadcast_to([S, NP, D]), ALU.mult) \
                          .then_inc(yt_ready, 1)

            def add_attention(i):
                dve.wait_ge(wo_done, i + 1)
                v_.tensor_tensor(xs[:, i], bank(2 if i < own_w else 5)[:, 0:C], xs[:, i], ALU.add).then_inc(x1_ready, 1)
                dve.wait_ge(x1_ready, i + 1)
                v_.bn_stats(stat2[:, i], xs[:, i]).then_inc(st2, 1)
                dve.wait_ge(st2, 2 * i + 1)
                v_.bn_aggr(mv2[:, i], stat2[:, i]).then_inc(st2, 1)
                dve.wait_ge(st2, 2 * i + 2)
                v_.tensor_scalar(mv2[:, i, 1:2], mv2[:, i, 1:2], EPS, None, ALU.add).then_inc(ag2, 1)

            def norm2(i):
                dve.wait_ge(rstd2_ready, i + 1)
                if i >= RB:
                    dve.wait_ge(xT_done, i - RB + 1)
                v_.tensor_scalar(x2n[:, i % RB], xs[:, i], mv2[:, i, 0:1], rstd2[:, i:i + 1],
                                 ALU.subtract, ALU.mult).then_inc(x2n_ready, 1)

            def read_logits(g):
                dve.wait_ge(log_done, TG * (g + 1))
                v_.tensor_copy(lgs[:, TG * g:TG * g + TG].rearrange("p t e -> p (t e)"),
                               bank(4)[:, LG:LG + TG * E]).then_inc(log_read, 1)

            steps = [0]

            def step(ins):
                steps[0] += 1
                ins.then_inc(routed, 1)
                dve.wait_ge(routed, steps[0])

            def over(a, shape, dim):
                return a.unsqueeze(dim).broadcast_to(shape)

            def route(r, part):
                g0, ng = ROUTE[r]
                n = TG * ng
                full = [P, n, E]
                g_t = [a[:, 0:n] for a in gt]
                t_t = [a[:, 0:n] for a in tt]
                g_s = [a[:, 0:n * NG] for a in gs]
                pr = [a[:, 0:n * NG] for a in pair]
                prob, score, kept = g_t[2], g_t[3], g_t[4]
                if part == 0:
                    assert steps[0] == route_base[r]
                    lg = lgs[:, TG * g0:TG * g0 + n]
                    dve.wait_ge(log_read, g0 + ng)
                    step(v_.tensor_reduce(t_t[0], lg, X, ALU.max))
                    step(v_.tensor_tensor(g_t[0], lg, over(t_t[0], full, 2), ALU.subtract))
                if part == 1:
                    dve.wait_ge(route_exp, r + 1)
                    step(v_.tensor_reduce(t_t[1], g_t[1], X, ALU.add))
                    step(v_.reciprocal(t_t[2], t_t[1]))
                    step(v_.tensor_tensor(prob, g_t[1], over(t_t[2], full, 2), ALU.mult))
                    step(v_.tensor_tensor(score, prob, over(gb, full, 1), ALU.add))
                if part == 2:
                    two = score.rearrange("p t (g k w) -> p (t g) k w", g=NG, w=2)
                    step(v_.tensor_tensor(pr[0], two[:, :, :, 0], two[:, :, :, 1], ALU.max))
                    step(v_.tensor_tensor(pr[1], two[:, :, :, 0], two[:, :, :, 1], ALU.min))
                    step(v_.tensor_tensor(g_s[0], pr[0][:, :, 0], pr[0][:, :, 1], ALU.max))
                    step(v_.tensor_tensor(g_s[1], pr[0][:, :, 0], pr[0][:, :, 1], ALU.min))
                    step(v_.tensor_tensor(g_s[2], pr[1][:, :, 0], pr[1][:, :, 1], ALU.max))
                    step(v_.tensor_tensor(g_s[3], g_s[1], g_s[2], ALU.max))
                    step(v_.tensor_tensor(g_s[4], g_s[0], g_s[3], ALU.add))
                if part == 3:
                    g4 = g_s[4].rearrange("p (t g) -> p t g", g=NG)
                    sq = [P, n, NG, NG]
                    other, own = over(g4, sq, 2), over(g4, sq, 3)
                    sqv = [g_t[k].rearrange("p t (a b) -> p t a b", b=NG) for k in (4, 5)]
                    step(v_.tensor_tensor(sqv[0], other, own, ALU.is_gt))
                    step(v_.tensor_tensor(sqv[1], other, own, ALU.is_equal))
                    step(v_.tensor_tensor(g_t[6], g_t[5], over(below, full, 1), ALU.mult))
                    step(v_.tensor_tensor(g_t[5], g_t[4], g_t[6], ALU.add))
                    step(v_.tensor_reduce(g_s[5].rearrange("p (t g) -> p t g", g=NG), sqv[1], X, ALU.add))
                    step(v_.tensor_scalar(g_s[0], g_s[5], 1.5, -BIG, ALU.is_gt, ALU.mult))
                    step(v_.tensor_tensor(kept.rearrange("p t (g k) -> p t g k", k=GE),
                                          score.rearrange("p t (g k) -> p t g k", k=GE),
                                          over(g_s[0].rearrange("p (t g) -> p t g", g=NG), [P, n, NG, GE], 3),
                                          ALU.add))

                def largest(src, sel, a, b, m1, m2):
                    step(v_.tensor_reduce(m1, src, X, ALU.max))
                    step(v_.tensor_tensor(a, src, over(m1, full, 2), ALU.is_equal))
                    step(v_.tensor_tensor(b, a, over(rev, full, 1), ALU.mult))
                    step(v_.tensor_reduce(m2, b, X, ALU.max))
                    step(v_.tensor_tensor(sel, b, over(m2, full, 2), ALU.is_equal))

                if part == 4:
                    largest(kept, g_t[0], g_t[5], g_t[6], t_t[3], t_t[4])
                    step(v_.scalar_tensor_tensor(out=g_t[1], in0=g_t[0], scalar=-BIGGER, in1=kept,
                                                 op0=ALU.mult, op1=ALU.add))
                if part == 5:
                    largest(g_t[1], g_t[3], g_t[5], g_t[6], t_t[5], t_t[6])
                    step(v_.tensor_tensor(g_t[5], g_t[0], g_t[3], ALU.add))
                    step(v_.tensor_tensor(g_t[6], g_t[5], prob, ALU.mult))
                    c = cc[:, TG * g0:TG * g0 + n]
                    step(v_.tensor_copy(hi16[:, 0:n], g_t[6]))
                    step(v_.tensor_copy(c[:, :, 0:E], hi16[:, 0:n]))
                    v_.tensor_tensor(c[:, :, E:2 * E], g_t[6], hi16[:, 0:n], ALU.subtract).then_inc(cc_ready, ng)

            def gated(u):
                n, j = unit(u)
                dve.wait_ge(H3_done, u + 1)
                dve.wait_ge(sil_ready, u + 1)
                if u == 0:
                    dve.wait_ge(qm_loaded[G - 1], 16 * HQ)
                if u >= 2:
                    dve.wait_ge(gl_ready, u - 1)
                dst = G32 if j == JE else U
                v_.scalar_tensor_tensor(out=dst[:, u % 2], in0=bank(pair_of(u)[0] + 1),
                                        scalar=pb[:, B_B3 + j:B_B3 + j + 1], in1=sil[:, u % 2],
                                        op0=ALU.add, op1=ALU.mult).then_inc(U_ready, 1)
                if j < JE:
                    dve.wait_ge(U_ready, u + 1)
                    dve.wait_ge(CR_done, n * JE + j + 1)
                    v_.tensor_tensor(G32[:, u % 2], bank(7), U[:, u % 2], ALU.mult).then_inc(G_ready, 1)

            def residual(n):
                dve.wait_ge(oT_done, n + 1)
                if n == 0:
                    for hb in range(2):
                        dve.wait_ge(ST_done[hb], T)
                if n >= 2:
                    dve.wait_ge(stored[n % 2], 16 * (n // 2))
                v_.tensor_tensor(ob[:, n % 2], bank(5), xs[:, n * TG:(n + 1) * TG].rearrange("p t c -> p (t c)"),
                                 ALU.add).then_inc(ob_ready, 1)

            for s in range(STEPS):
                for i in tile_at(s, "hi_values"):
                    hi_values(i)
                for i in tile_at(s, "lo_probs_d"):
                    lo_probs(i)
                for r in round_at(s, "route2"):
                    route(r, 2)
                for i in tile_at(s, "norm"):
                    norm(i)
                for i in tile_at(s, "rotate"):
                    rotate(i)
                for i in tile_at(s, "add_attention"):
                    add_attention(i)
                for i in tile_at(s, "norm2"):
                    norm2(i)
                for i in tile_at(s, "find_max"):
                    find_max(i)
                for i in tile_at(s, "divide"):
                    divide(i)
                for g in group_at(s, "read_logits"):
                    read_logits(g)
                for n in chunk_at(s, "residual"):
                    residual(n)
                for i in tile_at(s, "zero_qm0"):
                    zero_qm(i)
                for r in round_at(s, "route0"):
                    route(r, 0)
                for g in next_group_at(s, "nstats"):
                    norm_stats(g)
                for r in round_at(s, "route4"):
                    route(r, 4)
                for r in round_at(s, "route3"):
                    route(r, 3)
                for r in round_at(s, "route1"):
                    route(r, 1)
                for r in round_at(s, "route5"):
                    route(r, 5)
                for i in tile_at(s, "lo_values"):
                    lo_values(i)
                for u in unit_at(s, "gated"):
                    gated(u)

        @block.tensor
        def _(pe):
            t_ = nc.tensor

            def turn_tile(i):
                pe.wait_ge(xh_ready, i + 1)
                if i == 0:
                    pe.wait_ge(loaded_a, 16)
                if i % TG == 0:
                    pe.wait_ge(loaded_c[i // TG], 16)
                if i >= 2:
                    pe.wait_ge(xcT_ready, i - 1)
                t_.transpose(bank(i % 2)[:, 0:P], xh[:, i % 2], ident)
                t_.transpose(bank(i % 2)[:, P:2 * P], cs[:, i % (CR * TG)], ident).then_inc(T_done, 1)

            def project(i):
                pe.wait_ge(xcT_ready, i + 1)
                if i >= 2:
                    pe.wait_ge(rot_done, 2 * (i - 1))
                    pe.wait_ge(vl_ready, BT * (i - 1))
                t_.matmul(bank(2 + i % 2)[:, 0:C], xcT[:, i % 2, 0:P], wq, start=True, stop=True)
                t_.matmul(bank(2 + i % 2)[:, C:3 * C], xcT[:, i % 2, P:2 * P], wkv, start=True, stop=True) \
                  .then_inc(qkv_done, 1)

            def turn_stacks(i):
                pe.wait_ge(lo_ready, 2 * (i + 1))
                if i == 0:
                    pe.wait_ge(id16_ready, 1)
                if i >= 2:
                    pe.wait_ge(stk_ready, i - 1)
                for k in range(2 * NS):
                    last = t_.transpose(bank(4 + i % 2).bitcast(F16)[:, P * k:P * k + P],
                                        ex[:, i % 3, P * k:P * k + P], ident16[:])
                last.then_inc(stackT_done, 1)

            def maxima(t, b):
                g, tl = divmod(t, TG)
                if tl == 0 and b == 0:
                    pe.wait_ge(qm_loaded[g], 16 * HQ)
                if t >= 1:
                    pe.wait_ge(mx_ready, BT * (t - 1) + b + 1)
                if b == 1 and tl == 0 and g >= 1:
                    pe.wait_ge(mT_read, g)
                m = tl * BT + b
                for n in range(NP):
                    k, rh = divmod(n, 2)
                    two = QM[:, g % QR, k * TG * BT + m, 2 * rh:2 * rh + 2].rearrange("p h q -> p (h q)")
                    last = t_.matmul(bank(6 + b)[:, S * n:S * n + S], two, stk[:, g, k, S * m:S * m + S],
                                     start=True, stop=True)
                last.then_inc(S_done[b], 1)

            def turn_m(g):
                pe.wait_ge(mx_ready, BT * TG * (g + 1))
                t_.transpose(bank(7)[0:2 * NS * TG * BT, 0:P], mx[:, g], ident).then_inc(mT_done, 1)

            def turn(use):
                pe.wait_ge(*since(use))

            def scores(i, hb):
                g, tl = divmod(i, TG)
                if tl == 0:
                    pe.wait_ge(m_moved[g], 16 * HQ)
                if i == 0:
                    pe.wait_ge(xcT_ready, T)
                else:
                    pe.wait_ge(exp_ready[hb], i)
                for k in (2 * hb, 2 * hb + 1):
                    for b in range(BT):
                        m = tl * BT + b
                        c = HQ * S * (k % 2)
                        last = t_.matmul(bank(hb)[S * b:S * b + S, c:c + HQ * S], stk[:, g, k, S * m:S * m + S],
                                         QM[:, g % QR, k * TG * BT + m].rearrange("p h q -> p (h q)"),
                                         start=True, stop=True)
                last.then_inc(ST_done[hb], 1)

            def values(i):
                pe.wait_ge(pl_ready, i + 1)
                pe.wait_ge(pld_ready, i + 1)
                if i == 0:
                    pe.wait_ge(vl_ready, BT * T)
                    pe.wait_ge(stk_ready, T)
                if i >= 1:
                    pe.wait_ge(yt_ready, 4 * i)
                if tiles_before("logits", i + LAG["values"], False) >= TG:
                    pe.wait_ge(log_read, tiles_before("logits", i + LAG["values"], False) // TG)
                for n in range(NP):
                    o = bank(4)[:, VB * n:VB * n + VB]
                    c = slice(P * n, P * n + P)
                    t_.matmul(o, Ph[:, i % RP, c], Vh[:, i, n], start=True, stop=False)
                    t_.matmul(o, Ph[:, i % RP, c], Vl[:, i, n], start=False, stop=False)
                    last = t_.matmul(o, Pl[:, i % 2, c], Vh[:, i, n], start=False, stop=True)
                last.then_inc(pv_done, 1)

            def turn_y(i):
                turn(("y", i))
                pe.wait_ge(yt_ready, 4 * (i + 1))
                t_.transpose(bank(5)[:, 0:P], yt[:, i % RB], ident).then_inc(yT_done, 1)

            def project_out(i):
                if i >= own_w:
                    turn(("w", i))
                elif i == 0:
                    pe.wait_ge(rot_done, 2 * T)
                    pe.wait_ge(vl_ready, BT * T)
                else:
                    pe.wait_ge(x1_ready, i)
                pe.wait_ge(yT_ready, i + 1)
                if i == 0:
                    pe.wait_ge(loaded_b, 16)
                t_.matmul(bank(2 if i < own_w else 5)[:, 0:C], yT[:, i % RB], wo, start=True, stop=True).then_inc(wo_done, 1)

            def turn_x2(i):
                if i >= own_x:
                    turn(("x", i))
                elif i == 0:
                    pe.wait_ge(rot_done, 2 * T)
                    pe.wait_ge(vl_ready, BT * T)
                else:
                    pe.wait_ge(x2f_ready, i)
                pe.wait_ge(x2n_ready, i + 1)
                t_.transpose(bank(3 if i < own_x else 5)[:, 0:P], x2n[:, i % RB], ident).then_inc(xT_done, 1)

            def logits(i):
                pe.wait_ge(x2l_ready, i + 1)
                pe.wait_ge(wl_ready, 4)
                pe.wait_ge(yt_ready, 4 * tiles_before("values", i + LAG["logits"], True))
                if i % TG == 0 and i >= TG:
                    pe.wait_ge(log_read, i // TG)
                c = slice(P * i, P * i + P)
                o = bank(4)[:, LG + E * (i % TG):LG + E * (i % TG) + E]
                t_.matmul(o, x2h[:, c], gwh[:], start=True, stop=False)
                t_.matmul(o, x2h[:, c], gwl[:], start=False, stop=False)
                t_.matmul(o, x2l[:, c], gwh[:], start=False, stop=True).then_inc(log_done, 1)

            def split(o, n, j, mh, ml, start=True, stop=True):
                w = slice(P * j, P * j + P)
                t_.matmul(o, wh[n][:, w], mh, start=start, stop=False)
                t_.matmul(o, wh[n][:, w], ml, start=False, stop=False)
                return t_.matmul(o, wl[n][:, w], mh, start=False, stop=stop)

            def up(u):
                n, j = unit(u)
                c = slice(CH * n, CH * n + CH)
                pair, last = pair_of(u)
                if pair == 0 and last < 0:
                    for hb in range(2):
                        pe.wait_ge(exp_ready[hb], T)
                if pair == 2 and last < 0:
                    pe.wait_ge(x1_ready, own_w)
                    pe.wait_ge(x2f_ready, own_x)
                    pe.wait_ge(rot_done, 2 * T)
                    pe.wait_ge(vl_ready, BT * T)
                if j == JE:
                    pe.wait_ge(x2l_ready, TG * (n + 1))
                if last >= 0:
                    pe.wait_ge(sil_ready, last + 1)
                split(bank(pair), 0, j, x2h[:, c], x2l[:, c]).then_inc(H1_done, 1)
                if last >= 0:
                    pe.wait_ge(U_ready, last + 1)
                split(bank(pair + 1), 1, j, x2h[:, c], x2l[:, c]).then_inc(H3_done, 1)

            def spread(u):
                n, j = unit(u)
                v = n * JE + j
                if j == 0:
                    pe.wait_ge(cT_ready, n + 1)
                if v == 0:
                    pe.wait_ge(mT_read, G)
                    pe.wait_ge(mx_ready, BT * T)
                if v >= 1:
                    pe.wait_ge(G_ready, v)
                t_.matmul(bank(7), sel_r[:, P * j:P * j + P], cT[:, CH * n:CH * n + CH],
                          start=True, stop=True).then_inc(CR_done, 1)

            def down(u):
                n, j = unit(u)
                pe.wait_ge(gl_ready, u + 1)
                if j == JE and n == 0:
                    pe.wait_ge(mx_ready, BT * T)
                elif j == JE:
                    pe.wait_ge(yo_ready, n)
                split(bank(6), 2, j, Gh[:, u % 3], Gl[:, u % 3], start=j == JE, stop=False if j == JE else j == JE - 1)\
                    .then_inc(Y_part, 1)
                if j == 0:
                    c = slice(CH * n, CH * n + CH)
                    t_.matmul(bank(6), b2h[:], cT[:, c], start=False, stop=False)
                    t_.matmul(bank(6), b2l[:], cT[:, c], start=False, stop=False)

            def turn_c(n):
                turn(("c", n))
                pe.wait_ge(cc_ready, n + 1)
                for t in range(TG):
                    last = t_.transpose(bank(5)[0:2 * E, P * t:P * t + P], cc[:, n * TG + t], ident)
                last.then_inc(cT_done, 1)

            def turn_out(n):
                turn(("o", n))
                pe.wait_ge(yo_ready, n + 1)
                for t in range(TG):
                    last = t_.transpose(bank(5)[:, P * t:P * t + P], yo[:, n % 2, P * t:P * t + P], ident)
                last.then_inc(oT_done, 1)

            for s in range(STEPS):
                for n in chunk_at(s, "turn_out"):
                    turn_out(n)
                for i in tile_at(s, "maxima0"):
                    maxima(i, 0)
                for i in tile_at(s, "project_out"):
                    project_out(i)
                for i in tile_at(s, "scores1"):
                    scores(i, 1)
                for i in tile_at(s, "scores0"):
                    scores(i, 0)
                for i in tile_at(s, "turn_y"):
                    turn_y(i)
                for u in unit_at(s, "up"):
                    up(u)
                for i in tile_at(s, "maxima1"):
                    maxima(i, 1)
                for i in tile_at(s, "values"):
                    values(i)
                for i in tile_at(s, "turn_x2"):
                    turn_x2(i)
                for i in tile_at(s, "project"):
                    project(i)
                for i in tile_at(s, "turn_tile"):
                    turn_tile(i)
                for i in tile_at(s, "turn_stacks"):
                    turn_stacks(i)
                for n in routed_at(s, "turn_c"):
                    turn_c(n)
                for i in tile_at(s, "logits"):
                    logits(i)
                for g in group_at(s, "turn_m"):
                    turn_m(g)
                for u in unit_at(s, "spread"):
                    if unit(u)[1] < JE:
                        spread(u)
                for u in unit_at(s, "down"):
                    down(u)


def kernel(x, ctx_1024, L0_xattn_Wq, L0_xattn_Wk, L0_xattn_Wv, L0_xattn_Wo, L0_ffn_gate_w, L0_ffn_gate_b,
           L0_ffn_We1, L0_ffn_be1, L0_ffn_We2, L0_ffn_be2, L0_ffn_We3, L0_ffn_be3, L0_ffn_ws1, L0_ffn_bs1,
           L0_ffn_ws2, L0_ffn_bs2, L0_ffn_ws3, L0_ffn_bs3):
    import numpy as np
    import concourse.bacc as bacc
    from concourse.bass_utils import run_bass_kernel_spmd

    f = lambda a: np.asarray(a)
    freqs = 1.0 / 10000.0 ** (np.arange(0, C, 2, dtype=np.float32) / C)
    ang = np.outer(np.arange(S, dtype=np.float32), freqs.astype(np.float32)).astype(np.float32)
    cosv = np.tile(np.repeat(np.cos(ang), 2, 1), (BT, 1))
    sinv = np.tile(np.repeat(np.sin(ang), 2, 1) * np.tile([-1.0, 1.0], C // 2), (BT, 1))
    scale = 1.0 / np.sqrt(D)
    cos = np.concatenate([cosv * scale, cosv], 1).astype(np.float32)
    sin = np.concatenate([sinv * scale, sinv], 1).astype(np.float32)
    ident = np.eye(P, dtype=np.float32)
    below = np.tile(np.tril(np.ones((NG, NG), np.float32), -1).reshape(1, -1), (P, 1))
    rev = np.tile(np.arange(E, 0, -1, dtype=np.float32), (P, 1))
    sel = (np.arange(2 * E)[:, None] % E == np.arange(E * I)[None, :] // I).astype(np.float32)

    col = lambda be, bs: np.concatenate([f(be).reshape(JE, P).T, f(bs).reshape(P, 1)], 1)
    pack_a = np.concatenate([f(L0_xattn_Wq).T, f(L0_xattn_Wk).T, f(L0_xattn_Wv).T, cos, sin, ident], 1)
    pack_b = np.concatenate([f(L0_xattn_Wo).T, f(L0_ffn_gate_w).T, np.tile(f(L0_ffn_gate_b).reshape(1, E), (P, 1)),
                             col(L0_ffn_be1, L0_ffn_bs1), col(L0_ffn_be3, L0_ffn_bs3),
                             f(L0_ffn_bs2).reshape(P, 1), below, rev], 1)
    pack_k = np.concatenate([np.tile(f(L0_ffn_be2), (2, 1)), sel], 1)
    up = lambda we, ws: np.concatenate([f(we).transpose(1, 0, 2).reshape(C, E * I), f(ws)], 1)
    w2 = np.concatenate([f(L0_ffn_We2).reshape(JE, P, C).transpose(1, 0, 2).reshape(P, JE * C), f(L0_ffn_ws2)], 1)
    arrays = {
        "in_x": f(x).reshape(TOK, C), "in_ctx": f(ctx_1024).reshape(TOK, C), "in_a": pack_a, "in_b": pack_b,
        "in_k": pack_k, "in_w1": up(L0_ffn_We1, L0_ffn_ws1), "in_w3": up(L0_ffn_We3, L0_ffn_ws3), "in_w2": w2,
    }
    arrays = {k: np.ascontiguousarray(v) for k, v in arrays.items()}
    nc = bacc.Bacc("TRN2", target_bir_lowering=False, num_devices=1)
    args = [nc.dram_tensor(k, v.shape, mybir.dt.from_np(v.dtype), kind="ExternalInput").ap()
            for k, v in arrays.items()]
    args.append(nc.dram_tensor("out", (TOK, C), F32, kind="ExternalOutput").ap())
    program(nc, *args)
    r = run_bass_kernel_spmd(nc, [arrays], core_ids=[0])
    return r.results[0]["out"].reshape(B, S, C)
```

```python
from contextlib import ExitStack

import concourse.bass as bass
from concourse import mybir

F32 = mybir.dt.float32
F32R = mybir.dt.float32r
F16 = mybir.dt.float16
ALU = mybir.AluOpType
ACT = mybir.ActivationFunctionType
X = mybir.AxisListType.X

P = 128
C = 128
B, S = 32, 64
H, D = 16, 8
E, I = 16, 64
NG, GE = 4, 4
TOK = B * S
T = TOK // P
BT = P // S
HQ = 4
NS = H // HQ
ROW = P // HQ
MROW = 3 * D
TG = 4
G = T // TG
NP = H // 2
VW = D + 1
VB = BT * 2 * VW
QR = 3
CH = 512
NC = TOK // CH
J = E * I // P + 1
JE = J - 1
CR = 2
EPS = 1e-5
BIG = 1e30
BIGGER = 1e32

ROUTE = [(0, 1), (1, 1), (2, 2)]
ROUTE_STEPS = 35
RT = TG * max(n for _, n in ROUTE)
ZP = 4
STORE_LAG = 12
WR = 3
RP = 3
RB = 3

A_WQ, A_WK, A_WV, A_COS, A_SIN, A_ID = 0, 128, 256, 384, 640, 896
A_N = 1024
B_WO, B_GW, B_GB, B_B1, B_B3, B_S2, B_LT, B_REV = 0, 128, 144, 160, 169, 178, 179, 195
B_N = 211
K_N = C

LAG = {
    "scores1": 23, "maxima0": 16, "up": 43, "scores0": 23, "maxima1": 16, "down": 46, "values": 25,
    "turn_tile": 1, "project": 2, "turn_y": 26, "turn_out": 49, "turn_c": 42, "project_out": 27,
    "turn_stacks": 6, "turn_x2": 30, "turn_m": 16, "logits": 33,
    "silu": 43, "negate_m": 17, "store_turned": 1, "exp_logits": 35, "exps1": 23, "exps0": 23,
    "store_y": 48, "hi_probs": 23, "store_x1": 27, "store_yT": 26, "store_x2": 30, "store_stacks": 7,
    "weights_hi": 10, "hi_parts": 4, "hi_g": 44, "zero_qm": 0, "store_cT": 42,
    "route2": 36, "norm": 0, "rotate": 3, "find_max": 16, "divide": 25, "route4": 37, "norm2": 29,
    "hi_values": 3, "nstats": 2, "route3": 36, "gated": 43, "route1": 35, "lo_values": 3, "residual": 49,
    "read_logits": 33, "route0": 34, "stats2": 27, "route5": 37,
    "lo_g": 47, "lo_probs": 26, "add_rotated": 3, "lo_parts": 5, "lo_x2": 33, "deviation2": 30, "dev": 2,
    "weights_lo": 12,
}


def program(nc, x, ctx_in, pack_a, pack_b, pack_k, w1, w3, w2, out):
    with ExitStack() as st:
        def sb(name, shape, dt=F32):
            return st.enter_context(nc.sbuf_tensor(name, shape, dt))

        def sem(name):
            return st.enter_context(nc.semaphore(name))

        xs = sb("xs", [P, T, C])
        pa = sb("pa", [P, A_N])
        pb = sb("pb", [P, B_N])
        b2h = sb("b2h", [2 * E, C], F16)
        b2l = sb("b2l", [2 * E, C], F16)
        gwh = sb("gwh", [P, E], F32R)
        gwl = sb("gwl", [P, E], F32R)
        ident16 = sb("ident16", [P, P], F16)
        stat = sb("stat", [P, T, 6])
        mv = sb("mv", [P, T, 2])
        rstd = sb("rstd", [P, T])
        mhalf = sb("mhalf", [P, T])
        Vh = sb("Vh", [P, T, NP, VB], F16)
        Vl = sb("Vl", [P, T, NP, VB], F16)
        x2h = sb("x2h", [P, TOK], F32R)
        x2l = sb("x2l", [P, TOK], F32R)
        wh = [sb(f"w{n}h", [P, J * P], F32R) for n in (1, 3, 2)]
        wl = [sb(f"w{n}l", [P, J * P], F32R) for n in (1, 3, 2)]
        mx = sb("mx", [P, 2, 2 * NS * TG * BT])
        mneg = sb("mneg", [2 * NS * TG * BT, 2, P], F16)
        rsum = sb("rsum", [P, RB, NP * BT])
        yt = sb("yt", [P, RB, C])
        yT = sb("yT", [P, RB, P])
        x2n = sb("x2n", [P, RB, C])
        x2f = sb("x2f", [P, RB, P])
        shared = sb("shared", [P, max(3 * J * P + K_N, 3072 + 512 * RP)])
        pk = shared[0:2 * E, 3 * J * P:3 * J * P + K_N]
        wraw = [shared[:, n * J * P:(n + 1) * J * P] for n in range(3)]
        P32 = shared[:, 0:2048].rearrange("p (s m) -> p s m", s=2)
        Ph = shared[:, 2048:2048 + 512 * RP].bitcast(F16).rearrange("p (s m) -> p s m", s=RP)
        Pl = shared[:, 2048 + 512 * RP:3072 + 512 * RP].bitcast(F16).rearrange("p (s m) -> p s m", s=2)
        stk = sb("stk", [P, G, NS, TG * P], F16)
        cT = sb("cT", [2 * E, 2, CH], F16)
        c32 = sb("c32", [3 * E, 2, CH])
        lgs = sb("lgs", [P, T, E])
        gt = [sb(f"gt{n}", [P, RT, E]) for n in range(7)]
        pair = [sb(f"pair{n}", [P, RT * NG, 2]) for n in range(2)]
        gs = [sb(f"gs{n}", [P, RT * NG]) for n in range(6)]
        tt = [sb(f"tt{n}", [P, RT]) for n in range(7)]
        hi16 = sb("hi16", [P, RT, E], F16)
        cc = sb("cc", [P, T, 3 * E])

        with ExitStack() as early:
            def eb(name, shape, dt=F32):
                return early.enter_context(nc.sbuf_tensor(name, shape, dt))

            cs = eb("cs", [P, CR * TG, C])
            xh = eb("xh", [P, 2, C])
            xcT = eb("xcT", [P, 2, 2 * P])
            rt = eb("rt", [P, 2, 2, 2 * C])
            rs = eb("rs", [P, 3, 2 * C])
            ex = eb("ex", [P, 3, 2 * NS * P], F16)
            stq = eb("stq", [P, 2, NS, TG * P], F16)
            QM = eb("QM", [P, QR, NS * TG * BT, HQ, S], F16)
        sil = sb("sil", [P, 2, CH])
        U = sb("U", [P, 2, CH])
        G32 = sb("G32", [P, 2, CH])
        Gh = sb("Gh", [P, 3, CH], F32R)
        Gl = sb("Gl", [P, 2, CH], F32R)
        W = sb("W", [P, WR, CH])
        yo = sb("yo", [P, 2, CH])
        ob = sb("ob", [P, 2, CH])

        ps = st.enter_context(nc.psum_tensor("ps", [P, 8, 512], F32))

        def bank(n):
            return ps[:, n, :]

        wq = pa[:, A_WQ:A_WQ + C]
        wkv = pa[:, A_WK:A_WK + 2 * C]
        cos = pa[:, A_COS:A_COS + 2 * C]
        sin = pa[:, A_SIN:A_SIN + 2 * C]
        ident = pa[:, A_ID:A_ID + P]
        wo = pb[:, B_WO:B_WO + C]
        gb = pb[:, B_GB:B_GB + E]
        below = pb[:, B_LT:B_LT + NG * NG]
        rev = pb[:, B_REV:B_REV + E]

        loaded_a = sem("loaded_a")
        loaded_b = sem("loaded_b")
        loaded_k = sem("loaded_k")
        loaded_x = [sem(f"loaded_x{g}") for g in range(G)]
        loaded_c = [sem(f"loaded_c{g}") for g in range(G)]
        loaded_w = [sem(f"loaded_w{n}") for n in range(3)]
        qm_loaded = [sem(f"qm_loaded{g}") for g in range(G)]
        m_moved = [sem(f"m_moved{g}") for g in range(G)]
        stored = [sem(f"stored{n}") for n in range(2)]
        qm_zero = sem("qm_zero")
        ex_zero = sem("ex_zero")
        vh_zero = sem("vh_zero")
        vl_zero = sem("vl_zero")
        consts = sem("consts")
        id16_ready = sem("id16_ready")
        stats = sem("stats")
        mv_ready = sem("mv_ready")
        aggrs = sem("aggrs")
        rstds = sem("rstds")
        xh_ready = sem("xh_ready")
        T_done = sem("T_done")
        xcT_ready = sem("xcT_ready")
        qkv_done = sem("qkv_done")
        rot_done = sem("rot_done")
        rs_ready = sem("rs_ready")
        hi_ready = sem("hi_ready")
        lo_ready = sem("lo_ready")
        vh_ready = sem("vh_ready")
        vl_ready = sem("vl_ready")
        stackT_done = sem("stackT_done")
        stk_ready = sem("stk_ready")
        wh_ready = sem("wh_ready")
        wl_ready = sem("wl_ready")
        S_done = [sem(f"S_done{n}") for n in range(2)]
        mx_ready = sem("mx_ready")
        mT_done = sem("mT_done")
        mT_read = sem("mT_read")
        ST_done = [sem(f"ST_done{n}") for n in range(2)]
        exp_ready = [sem(f"exp_ready{n}") for n in range(2)]
        ph_ready = sem("ph_ready")
        pl_ready = sem("pl_ready")
        pv_done = sem("pv_done")
        rsum_ready = sem("rsum_ready")
        yt_ready = sem("yt_ready")
        yT_done = sem("yT_done")
        yT_ready = sem("yT_ready")
        wo_done = sem("wo_done")
        x1_ready = sem("x1_ready")
        st2 = sem("st2")
        ag2 = sem("ag2")
        rstd2_ready = sem("rstd2_ready")
        x2n_ready = sem("x2n_ready")
        xT_done = sem("xT_done")
        x2f_ready = sem("x2f_ready")
        x2h_ready = sem("x2h_ready")
        x2l_ready = sem("x2l_ready")
        log_done = sem("log_done")
        log_read = sem("log_read")
        routed = sem("routed")
        route_exp = sem("route_exp")
        cc_ready = sem("cc_ready")
        cT_done = sem("cT_done")
        cT_ready = sem("cT_ready")
        H1_done = sem("H1_done")
        H3_done = sem("H3_done")
        spread_done = [sem(f"spread_done{n}") for n in range(WR)]
        sil_ready = sem("sil_ready")
        U_ready = sem("U_ready")
        G_ready = sem("G_ready")
        gh_ready = sem("gh_ready")
        gl_ready = sem("gl_ready")
        Y_part = sem("Y_part")
        yo_ready = sem("yo_ready")
        oT_done = sem("oT_done")
        ob_ready = sem("ob_ready")

        UNITS = [(n, j) for n in range(NC) for j in (JE, *range(JE))]
        UN = len(UNITS)
        before_experts = [UNITS.index((n, 0)) - 1 for n in range(NC)]
        last_unit = [UNITS.index((n, JE - 1)) for n in range(NC)]
        STEPS = max(LAG[n] for n in ("turn_out", "residual", "store_y", "down", "lo_g", "hi_g")) + UN

        def met(s, what, count):
            i = s - LAG[what]
            return [i] if 0 <= i < count else []

        def tile_at(s, what):
            return met(s, what, T)

        def unit_at(s, what):
            return met(s, what, UN)

        def group_at(s, what):
            return [i // TG for i in met(s, what, T) if i % TG == TG - 1]

        def next_group_at(s, what):
            return [i // TG + 1 for i in met(s, what, T) if i % TG == 0 and i // TG + 1 < G]

        def chunk_at(s, what):
            return [last_unit.index(i) for i in met(s, what, UN) if i in last_unit]

        def round_at(s, what):
            return [r for i in met(s, what, T) for r, (g, n) in enumerate(ROUTE) if i == TG * (g + n) - 1]

        def experts_at(s, what):
            return [before_experts.index(i) for i in met(s, what, UN) if i in before_experts]

        def unit(u):
            return UNITS[u]

        early_units = max(0, LAG["scores1"] + T - LAG["up"])

        def pair_of(u):
            if u < early_units:
                return 2, u - 1
            if (u - early_units) % 2 == 0:
                return 0, (u - 2 if u > early_units else -1)
            return 2, (u - 2 if u > early_units + 1 else early_units - 1)

        route_base = [ROUTE_STEPS * r for r in range(len(ROUTE))]

        own_w = min(T, max(0, LAG["up"] - LAG["project_out"]))
        own_x = min(T, max(0, LAG["up"] - LAG["turn_x2"]))

        def tiles_before(what, s, same):
            return max(0, min(T, s - LAG[what] + (1 if same else 0)))

        turns = []
        for s in range(STEPS):
            turns += [("y", i) for i in tile_at(s, "turn_y")]
            turns += [("o", n) for n in chunk_at(s, "turn_out")]
            turns += [("c", n) for n in experts_at(s, "turn_c")]
            turns += [("x", i) for i in tile_at(s, "turn_x2") if i >= own_x]

        def since(use):
            n = turns.index(use)
            if n == 0:
                return stk_ready, T
            what, k = turns[n - 1]
            return {"y": (yT_ready, k + 1), "x": (x2f_ready, k + 1),
                    "c": (cT_ready, k + 1), "o": (ob_ready, k + 1)}[what]

        LG = NP * VB

        x_v = x.rearrange("(g t p) c -> g p t c", g=G, p=P)
        c_v = ctx_in.rearrange("(g t p) c -> g p t c", g=G, p=P)
        o_v = out.rearrange("(n t p) c -> n p t c", n=NC, p=P)

        block = st.enter_context(nc.Block())

        @block.sync
        def _(sp):
            sp.dma_start(xs[:, 0:TG, :], x_v[0]).then_inc(loaded_x[0], 16)
            sp.dma_start(pa[:], pack_a).then_inc(loaded_a, 16)
            sp.dma_start(cs[:, 0:TG, :], c_v[0]).then_inc(loaded_c[0], 16)
            for g in range(1, G):
                sp.dma_start(xs[:, g * TG:(g + 1) * TG, :], x_v[g]).then_inc(loaded_x[g], 16)
                if g < CR:
                    sp.dma_start(cs[:, g * TG:(g + 1) * TG, :], c_v[g]).then_inc(loaded_c[g], 16)
            sp.dma_start(pb[:], pack_b).then_inc(loaded_b, 16)
            for n, w in enumerate((w1, w3, w2)):
                sp.dma_start(wraw[n], w).then_inc(loaded_w[n], 16)
            sp.dma_start(pk, pack_k).then_inc(loaded_k, 16)

            def load_c(g):
                sp.wait_ge(T_done, (g - CR + 1) * TG)
                slot = g % CR * TG
                sp.dma_start(cs[:, slot:slot + TG, :], c_v[g]).then_inc(loaded_c[g], 16)

            def load_qm(g):
                sp.wait_ge(stk_ready, (g + 1) * TG)
                sp.wait_ge(qm_zero, ZP * (min(g, QR - 1) + 1))
                if g >= QR:
                    for hb in range(2):
                        sp.wait_ge(ST_done[hb], TG * (g - QR + 1))
                for r in range(HQ):
                    rows = slice(ROW * r, ROW * r + ROW)
                    sp.dma_start(QM[rows, g % QR, :, r, :],
                                 stq[rows, g % 2].rearrange("p s (m q) -> p (s m) q", q=S)) \
                        .then_inc(qm_loaded[g], 16)

            def move_m(g):
                sp.wait_ge(mT_read, g + 1)
                half = NS * TG * BT
                for r in range(HQ):
                    rh, r2 = divmod(r, 2)
                    row = ROW * r + MROW
                    sp.dma_start(QM[row:row + 1, g % QR, :, r, :],
                                 mneg[half * rh:half * rh + half, g % 2, S * r2:S * r2 + S]) \
                        .then_inc(m_moved[g], 16)

            load_c(2)
            load_c(3)
            for g in range(QR):
                load_qm(g)
            move_m(0)
            move_m(1)
            for g in range(QR, G):
                load_qm(g)
                move_m(g - 1)
            move_m(G - 1)

            def spread(u):
                n, j = unit(u)
                v = n * JE + j
                if j == 0:
                    sp.wait_ge(cT_ready, n + 1)
                if v == 0:
                    sp.wait_ge(qm_loaded[G - 1], 16 * HQ)
                if v >= WR:
                    sp.wait_ge(G_ready, v - WR + 1)
                for e in range(P // I):
                    row = 2 * E + (P // I) * j + e
                    sp.dma_start(W[I * e:I * e + I, v % WR],
                                 c32[row:row + 1, n % 2].unsqueeze(1).broadcast_to([1, I, CH])) \
                        .then_inc(spread_done[v % WR], 16)

            def store(n):
                sp.wait_ge(ob_ready, n + 1)
                sp.dma_start(o_v[n], ob[:, n % 2, :].rearrange("p (t c) -> p t c", c=C)) \
                    .then_inc(stored[n % 2], 16)

            for u in range(UN + STORE_LAG):
                if u < UN and unit(u)[1] < JE:
                    spread(u)
                done = u - STORE_LAG
                if done in last_unit:
                    store(last_unit.index(done))
            for n in range(2):
                sp.wait_ge(stored[n], 16 * (NC // 2))

        @block.gpsimd
        def _(pool):
            g_ = nc.gpsimd
            g_.memset(mhalf[:], -0.5).then_inc(consts, 1)

            def deviations(g):
                pool.wait_ge(consts, 1)
                pool.wait_ge(aggrs, (g + 1) * TG)
                c = slice(g * TG, (g + 1) * TG)
                g_.tensor_tensor(rstd[:, c], mv[:, c, 1], mhalf[:, 0:TG], ALU.pow).then_inc(rstds, 1)

            def add_rotated(i):
                pool.wait_ge(rot_done, 2 * (i + 1))
                if i >= 3:
                    pool.wait_ge(lo_ready, 2 * (i - 2))
                g_.tensor_tensor(rs[:, i % 3], rt[:, i % 2, 0], rt[:, i % 2, 1], ALU.add).then_inc(rs_ready, 1)

            def lo_parts(i):
                pool.wait_ge(hi_ready, i + 1)
                pool.wait_ge(rs_ready, i + 1)
                o = ex[:, i % 3].rearrange("p (s h w) -> p s h w", s=2, w=ROW)
                src = rs[:, i % 3].rearrange("p (s h w) -> p s h w", s=2, w=D)
                g_.tensor_tensor(o[:, 0, :, 0:D], src[:, 0], o[:, 0, :, D:2 * D], ALU.subtract) \
                  .then_inc(lo_ready, 1)
                g_.tensor_tensor(o[:, 1, :, 2 * D:3 * D], src[:, 1], o[:, 1, :, D:2 * D], ALU.subtract) \
                  .then_inc(lo_ready, 1)

            def weight_lo(n):
                pool.wait_ge(wh_ready, n + 1)
                g_.tensor_tensor(wl[n][:], wraw[n], wh[n][:].bitcast(F32), ALU.subtract).then_inc(wl_ready, 1)

            deviations(0)
            for b in range(BT):
                if b == 0:
                    pool.wait_ge(vh_zero, 1)
                else:
                    pool.wait_ge(vh_zero, 1 + b)
                ones = Vh[S * b:S * b + S].rearrange("p t n (b h w) -> p (t n) b h w", b=BT, w=VW)
                g_.memset(ones[:, :, b, :, D], 1.0).then_inc(vh_zero, 1)
            pool.wait_ge(vh_zero, 1 + BT)

            def weights(i):
                if i >= 0 and i % 3 == 0 and i < 9:
                    weight_lo(i // 3)
                if i == 9:
                    pool.wait_ge(wh_ready, 5)
                    g_.tensor_tensor(gwl[:], pb[:, B_GW:B_GW + E], gwh[:].bitcast(F32), ALU.subtract) \
                      .then_inc(wl_ready, 1)
                    g_.tensor_tensor(b2l[:], pk, b2h[:], ALU.subtract).then_inc(wl_ready, 1)

            def lo_probs(i):
                pool.wait_ge(ph_ready, i + 1)
                if i >= 2:
                    pool.wait_ge(pv_done, i - 1)
                g_.tensor_tensor(Pl[:, i % 2], P32[:, i % 2], Ph[:, i % RP], ALU.subtract).then_inc(pl_ready, 1)

            def deviation2(i):
                pool.wait_ge(ag2, i + 1)
                g_.tensor_tensor(rstd[:, i:i + 1], mv[:, i, 1:2], mhalf[:, 0:1], ALU.pow) \
                  .then_inc(rstd2_ready, 1)

            def lo_x2(i):
                pool.wait_ge(x2h_ready, i + 1)
                c = slice(P * i, P * i + P)
                g_.tensor_tensor(x2l[:, c], x2f[:, i % RB], x2h[:, c].bitcast(F32), ALU.subtract) \
                  .then_inc(x2l_ready, 1)

            def lo_g(u):
                pool.wait_ge(gh_ready, u + 1)
                if u >= 2:
                    pool.wait_ge(Y_part, u - 1)
                g_.tensor_tensor(Gl[:, u % 2], G32[:, u % 2], Gh[:, u % 3].bitcast(F32), ALU.subtract) \
                  .then_inc(gl_ready, 1)

            for s in range(STEPS):
                for u in unit_at(s, "lo_g"):
                    lo_g(u)
                for i in tile_at(s, "lo_probs"):
                    lo_probs(i)
                for i in tile_at(s, "add_rotated"):
                    add_rotated(i)
                for i in tile_at(s, "lo_parts"):
                    lo_parts(i)
                for i in tile_at(s, "lo_x2"):
                    lo_x2(i)
                for i in tile_at(s, "deviation2"):
                    deviation2(i)
                for g in next_group_at(s, "dev"):
                    deviations(g)
                for i in tile_at(s, "weights_lo"):
                    weights(i)

        @block.scalar
        def _(act):
            a_ = nc.scalar
            a_.memzero(Vh[:].rearrange("p t n w -> p (t n w)").bitcast(F32)).then_inc(vh_zero, 1)
            a_.memzero(Vl[:].rearrange("p t n w -> p (t n w)").bitcast(F32)).then_inc(vl_zero, 1)
            act.wait_ge(loaded_a, 16)
            a_.copy(ident16[:], ident).then_inc(id16_ready, 1)

            def store_stacks(i):
                act.wait_ge(stackT_done, i + 1)
                g, c = i // TG, slice(P * (i % TG), P * (i % TG) + P)
                src = bank(4 + i % 2).bitcast(F16).rearrange("p (k s m) -> p k s m", k=2, s=NS)
                if i % TG == 0 and g >= 2:
                    act.wait_ge(qm_loaded[g - 2], 16 * HQ)
                a_.copy(stq[:, g % 2, :, c], src[:, 0])
                a_.copy(stk[:, g, :, c], src[:, 1]).then_inc(stk_ready, 1)

            def store_turned(i):
                act.wait_ge(T_done, i + 1)
                if i >= 2:
                    act.wait_ge(qkv_done, i - 1)
                a_.copy(xcT[:, i % 2], bank(i % 2)[:, 0:2 * P]).then_inc(xcT_ready, 1)

            def hi_parts(i):
                act.wait_ge(rs_ready, i + 1)
                if i == 0:
                    act.wait_ge(ex_zero, 2)
                if i >= 3:
                    act.wait_ge(stackT_done, i - 2)
                o = ex[:, i % 3].rearrange("p (s h w) -> p s h w", s=2, w=ROW)
                src = rs[:, i % 3].rearrange("p (s h w) -> p s h w", s=2, w=D)
                for side, first in ((0, D), (1, 0)):
                    dst = o[:, side, :, first:first + 2 * D].rearrange("p h (k w) -> p h k w", k=2)
                    last = a_.copy(dst, src[:, side].unsqueeze(2).broadcast_to([P, H, 2, D]))
                last.then_inc(hi_ready, 1)

            def zero_qm(i):
                n = NS * TG * BT // ZP
                q, k = i // ZP, slice(n * (i % ZP), n * (i % ZP + 1))
                a_.memzero(QM[:, q, k].rearrange("p m h q -> p (m h q)").bitcast(F32)).then_inc(qm_zero, 1)

            def weight_hi(n):
                act.wait_ge(loaded_w[n], 16)
                a_.copy(wh[n][:], wraw[n]).then_inc(wh_ready, 1)

            def negate_m(g):
                act.wait_ge(mT_done, g + 1)
                if g >= 2:
                    act.wait_ge(m_moved[g - 2], 16 * HQ)
                rows = 2 * NS * TG * BT
                a_.mul(mneg[:, g % 2, :], bank(7)[0:rows, 0:P], -1.0).then_inc(mT_read, 1)

            def weights(i):
                if i >= 0 and i % 3 == 0 and i < 9:
                    weight_hi(i // 3)
                if i == 9:
                    act.wait_ge(loaded_b, 16)
                    a_.copy(gwh[:], pb[:, B_GW:B_GW + E]).then_inc(wh_ready, 1)
                    act.wait_ge(loaded_k, 16)
                    a_.copy(b2h[:], pk).then_inc(wh_ready, 1)

            def exps(i, hb):
                act.wait_ge(ST_done[hb], i + 1)
                if i == 0:
                    act.wait_ge(wl_ready, 5)
                if i >= 2:
                    act.wait_ge(pl_ready, i - 1)
                a_.activation(P32[:, i % 2, 512 * hb:512 * hb + 512], bank(hb), ACT.Exp).then_inc(exp_ready[hb], 1)

            def hi_probs(i):
                for hb in range(2):
                    act.wait_ge(exp_ready[hb], i + 1)
                if i >= RP:
                    act.wait_ge(pv_done, i - RP + 1)
                a_.copy(Ph[:, i % RP], P32[:, i % 2]).then_inc(ph_ready, 1)

            def store_yT(i):
                act.wait_ge(yT_done, i + 1)
                if i >= RB:
                    act.wait_ge(wo_done, i - RB + 1)
                a_.copy(yT[:, i % RB], bank(5)[:, 0:P]).then_inc(yT_ready, 1)

            def store_x2(i):
                act.wait_ge(xT_done, i + 1)
                if i >= RB:
                    act.wait_ge(x2l_ready, i - RB + 1)
                a_.copy(x2f[:, i % RB], bank(3 if i < own_x else 5)[:, 0:P]).then_inc(x2f_ready, 1)
                act.wait_ge(x2f_ready, i + 1)
                a_.copy(x2h[:, P * i:P * i + P], x2f[:, i % RB]).then_inc(x2h_ready, 1)

            def store_x1(i):
                act.wait_ge(wo_done, i + 1)
                a_.copy(xs[:, i], bank(2 if i < own_w else 7)[:, 0:C]).then_inc(x1_ready, 1)

            def exp_logits(r):
                act.wait_ge(routed, route_base[r] + 2)
                n = TG * ROUTE[r][1]
                a_.activation(gt[1][:, 0:n], gt[0][:, 0:n], ACT.Exp).then_inc(route_exp, 1)

            def silu(u):
                n, j = unit(u)
                act.wait_ge(H1_done, u + 1)
                if u >= 2:
                    act.wait_ge(U_ready, u - 1)
                a_.activation(sil[:, u % 2], bank(pair_of(u)[0]), ACT.Silu, bias=pb[:, B_B1 + j:B_B1 + j + 1]) \
                  .then_inc(sil_ready, 1)

            def hi_g(u):
                n, j = unit(u)
                if j == JE:
                    act.wait_ge(U_ready, u + 1)
                else:
                    act.wait_ge(G_ready, n * JE + j + 1)
                if u >= 3:
                    act.wait_ge(Y_part, u - 2)
                a_.copy(Gh[:, u % 3], G32[:, u % 2]).then_inc(gh_ready, 1)

            def store_cT(n):
                act.wait_ge(cT_done, n + 1)
                if n >= 2:
                    act.wait_ge(Y_part, last_unit[n - 2] + 1)
                    act.wait_ge(G_ready, JE * (n - 1))
                a_.copy(cT[:, n % 2], bank(5)[0:2 * E, :])
                a_.copy(c32[2 * E:3 * E, n % 2], bank(5)[2 * E:3 * E, :]).then_inc(cT_ready, 1)

            def store_y(n):
                act.wait_ge(Y_part, last_unit[n] + 1)
                if n == 0:
                    for hb in range(2):
                        act.wait_ge(ST_done[hb], T)
                if n >= 2:
                    act.wait_ge(oT_done, n - 1)
                a_.activation(yo[:, n % 2], bank(6 + n % 2), ACT.Identity, bias=pb[:, B_S2:B_S2 + 1]) \
                  .then_inc(yo_ready, 1)

            for s in range(STEPS):
                for u in unit_at(s, "silu"):
                    silu(u)
                for g in group_at(s, "negate_m"):
                    negate_m(g)
                for i in tile_at(s, "store_turned"):
                    store_turned(i)
                for r in round_at(s, "exp_logits"):
                    exp_logits(r)
                for i in tile_at(s, "exps1"):
                    exps(i, 1)
                for i in tile_at(s, "exps0"):
                    exps(i, 0)
                for n in chunk_at(s, "store_y"):
                    store_y(n)
                for i in tile_at(s, "hi_probs"):
                    hi_probs(i)
                for i in tile_at(s, "store_x1"):
                    store_x1(i)
                for i in tile_at(s, "store_yT"):
                    store_yT(i)
                for i in tile_at(s, "store_x2"):
                    store_x2(i)
                for i in tile_at(s, "store_stacks"):
                    store_stacks(i)
                for i in tile_at(s, "weights_hi"):
                    weights(i)
                for i in tile_at(s, "hi_parts"):
                    hi_parts(i)
                for u in unit_at(s, "hi_g"):
                    hi_g(u)
                for i in met(s, "zero_qm", ZP * QR):
                    zero_qm(i)
                for n in experts_at(s, "store_cT"):
                    store_cT(n)

        @block.vector
        def _(dve):
            v_ = nc.vector
            v_.memset(ex[:].rearrange("p s w -> p (s w)").bitcast(F32), 0.0).then_inc(ex_zero, 1)
            dve.wait_ge(ex_zero, 1)
            keys = ex[:].rearrange("p k (s h w) -> p k s h w", s=2, w=ROW)
            v_.memset(keys[:, :, 1, :, MROW], 1.0).then_inc(ex_zero, 1)

            def norm_stats(g):
                dve.wait_ge(loaded_x[g], 16)
                for t in range(g * TG, (g + 1) * TG):
                    v_.bn_stats(stat[:, t], xs[:, t]).then_inc(stats, 1)
                for t in range(g * TG, (g + 1) * TG):
                    dve.wait_ge(stats, t + 1)
                    v_.bn_aggr(mv[:, t], stat[:, t]).then_inc(mv_ready, 1)
                dve.wait_ge(mv_ready, (g + 1) * TG)
                v = mv[:, g * TG:(g + 1) * TG, 1]
                v_.tensor_scalar(v, v, EPS, None, ALU.add).then_inc(aggrs, TG)

            def norm(i):
                dve.wait_ge(rstds, i // TG + 1)
                if i >= 2:
                    dve.wait_ge(T_done, i - 1)
                v_.tensor_scalar(xh[:, i % 2], xs[:, i], mv[:, i, 0:1], rstd[:, i:i + 1],
                                 ALU.subtract, ALU.mult).then_inc(xh_ready, 1)

            def rotate(i):
                dve.wait_ge(qkv_done, i + 1)
                if i >= 2:
                    dve.wait_ge(rs_ready, i - 1)
                if i == 0:
                    dve.wait_ge(loaded_a, 16)
                qk = bank(2 + i % 2)[:, 0:2 * C]
                v_.tensor_tensor(rt[:, i % 2, 0], qk, cos, ALU.mult).then_inc(rot_done, 1)
                swapped = qk.rearrange("p (m w) -> p m w", w=2)[:, :, ::-1]
                v_.tensor_tensor(rt[:, i % 2, 1].rearrange("p (m w) -> p m w", w=2), swapped,
                                 sin.rearrange("p (m w) -> p m w", w=2), ALU.mult).then_inc(rot_done, 1)

            def hi_values(i):
                dve.wait_ge(qkv_done, i + 1)
                if i == 0:
                    dve.wait_ge(vh_zero, 1 + BT)
                for b in range(BT):
                    rows = slice(S * b, S * b + S)
                    src = bank(2 + i % 2)[rows, 2 * C:3 * C].rearrange("p (n h w) -> p n h w", h=2, w=D)
                    dst = Vh[rows, i].rearrange("p n (b h w) -> p n b h w", b=BT, w=VW)
                    v_.tensor_copy(dst[:, :, b, :, 0:D], src).then_inc(vh_ready, 1)

            def lo_values(i):
                dve.wait_ge(vh_ready, BT * (i + 1))
                if i == 0:
                    dve.wait_ge(vl_zero, 1)
                for b in range(BT):
                    rows = slice(S * b, S * b + S)
                    src = bank(2 + i % 2)[rows, 2 * C:3 * C].rearrange("p (n h w) -> p n h w", h=2, w=D)
                    hi = Vh[rows, i].rearrange("p n (b h w) -> p n b h w", b=BT, w=VW)
                    lo = Vl[rows, i].rearrange("p n (b h w) -> p n b h w", b=BT, w=VW)
                    v_.tensor_tensor(lo[:, :, b, :, 0:D], src, hi[:, :, b, :, 0:D], ALU.subtract) \
                      .then_inc(vl_ready, 1)

            def find_max(t):
                g, tl = divmod(t, TG)
                if tl == 0 and g >= 2:
                    dve.wait_ge(mT_done, g - 1)
                for b in range(BT):
                    dve.wait_ge(S_done[b], t + 1)
                    dst = mx[:, g % 2].rearrange("p (r s m) -> p s r m", r=2, s=NS)[:, :, :, tl * BT + b]
                    v_.tensor_reduce(dst, bank(6 + b).rearrange("p (s r k) -> p s r k", s=NS, r=2), X, ALU.max) \
                      .then_inc(mx_ready, 1)

            norm_stats(0)
            def divide(i):
                dve.wait_ge(pv_done, i + 1)
                o = bank(4)[:, 0:NP * VB].rearrange("p (n b h w) -> p n b h w", b=BT, h=2, w=VW)
                v_.reciprocal(rsum[:, i % RB].rearrange("p (n b) -> p n b", b=BT), o[:, :, :, 0, D]) \
                  .then_inc(rsum_ready, 1)
                dve.wait_ge(rsum_ready, i + 1)
                if i >= RB:
                    dve.wait_ge(yT_done, i - RB + 1)
                for h2 in range(2):
                    for b in range(BT):
                        rows = slice(S * h2, S * h2 + S)
                        rr = rsum[rows, i % RB].rearrange("p (n b) -> p n b", b=BT)[:, :, b]
                        dst = yt[S * b:S * b + S, i % RB].rearrange("p (n h w) -> p n h w", h=2, w=D)
                        v_.tensor_tensor(dst[:, :, h2], o[rows, :, b, h2, 0:D],
                                         rr.unsqueeze(2).broadcast_to([S, NP, D]), ALU.mult) \
                          .then_inc(yt_ready, 1)

            def stats2(i):
                dve.wait_ge(x1_ready, i + 1)
                v_.bn_stats(stat[:, i], xs[:, i]).then_inc(st2, 1)
                dve.wait_ge(st2, 2 * i + 1)
                v_.bn_aggr(mv[:, i], stat[:, i]).then_inc(st2, 1)
                dve.wait_ge(st2, 2 * i + 2)
                v_.tensor_scalar(mv[:, i, 1:2], mv[:, i, 1:2], EPS, None, ALU.add).then_inc(ag2, 1)

            def norm2(i):
                dve.wait_ge(rstd2_ready, i + 1)
                if i >= RB:
                    dve.wait_ge(xT_done, i - RB + 1)
                v_.tensor_scalar(x2n[:, i % RB], xs[:, i], mv[:, i, 0:1], rstd[:, i:i + 1],
                                 ALU.subtract, ALU.mult).then_inc(x2n_ready, 1)

            def read_logits(g):
                dve.wait_ge(log_done, TG * (g + 1))
                v_.tensor_copy(lgs[:, TG * g:TG * g + TG].rearrange("p t e -> p (t e)"),
                               bank(4)[:, LG:LG + TG * E]).then_inc(log_read, 1)

            steps = [0]

            def step(ins, then_wait=True):
                steps[0] += 1
                ins.then_inc(routed, 1)
                if then_wait:
                    dve.wait_ge(routed, steps[0])

            def over(a, shape, dim):
                return a.unsqueeze(dim).broadcast_to(shape)

            def route(r, part):
                g0, ng = ROUTE[r]
                n = TG * ng
                full = [P, n, E]
                g_t = [a[:, 0:n] for a in gt]
                t_t = [a[:, 0:n] for a in tt]
                g_s = [a[:, 0:n * NG] for a in gs]
                pr = [a[:, 0:n * NG] for a in pair]
                prob, score, kept = g_t[2], g_t[3], g_t[4]
                if part == 0:
                    assert steps[0] == route_base[r]
                    lg = lgs[:, TG * g0:TG * g0 + n]
                    dve.wait_ge(log_read, g0 + ng)
                    step(v_.tensor_reduce(t_t[0], lg, X, ALU.max))
                    step(v_.tensor_tensor(g_t[0], lg, over(t_t[0], full, 2), ALU.subtract))
                if part == 1:
                    dve.wait_ge(route_exp, r + 1)
                    step(v_.tensor_reduce(t_t[1], g_t[1], X, ALU.add))
                    step(v_.reciprocal(t_t[2], t_t[1]))
                    step(v_.tensor_tensor(prob, g_t[1], over(t_t[2], full, 2), ALU.mult))
                    step(v_.tensor_tensor(score, prob, over(gb, full, 1), ALU.add))
                if part == 2:
                    two = score.rearrange("p t (g k w) -> p (t g) k w", g=NG, w=2)
                    step(v_.tensor_tensor(pr[0], two[:, :, :, 0], two[:, :, :, 1], ALU.max), then_wait=False)
                    step(v_.tensor_tensor(pr[1], two[:, :, :, 0], two[:, :, :, 1], ALU.min))
                    step(v_.tensor_tensor(g_s[0], pr[0][:, :, 0], pr[0][:, :, 1], ALU.max), then_wait=False)
                    step(v_.tensor_tensor(g_s[1], pr[0][:, :, 0], pr[0][:, :, 1], ALU.min), then_wait=False)
                    step(v_.tensor_tensor(g_s[2], pr[1][:, :, 0], pr[1][:, :, 1], ALU.max))
                    step(v_.tensor_tensor(g_s[3], g_s[1], g_s[2], ALU.max))
                    step(v_.tensor_tensor(g_s[4], g_s[0], g_s[3], ALU.add))
                if part == 3:
                    g4 = g_s[4].rearrange("p (t g) -> p t g", g=NG)
                    sq = [P, n, NG, NG]
                    other, own = over(g4, sq, 2), over(g4, sq, 3)
                    sqv = [g_t[k].rearrange("p t (a b) -> p t a b", b=NG) for k in (4, 5)]
                    step(v_.tensor_tensor(sqv[0], other, own, ALU.is_gt), then_wait=False)
                    step(v_.tensor_tensor(sqv[1], other, own, ALU.is_equal))
                    step(v_.tensor_tensor(g_t[6], g_t[5], over(below, full, 1), ALU.mult))
                    step(v_.tensor_tensor(g_t[5], g_t[4], g_t[6], ALU.add))
                    step(v_.tensor_reduce(g_s[5].rearrange("p (t g) -> p t g", g=NG), sqv[1], X, ALU.add))
                    step(v_.tensor_scalar(g_s[0], g_s[5], 1.5, -BIG, ALU.is_gt, ALU.mult))
                    step(v_.tensor_tensor(kept.rearrange("p t (g k) -> p t g k", k=GE),
                                          score.rearrange("p t (g k) -> p t g k", k=GE),
                                          over(g_s[0].rearrange("p (t g) -> p t g", g=NG), [P, n, NG, GE], 3),
                                          ALU.add))

                def largest(src, sel, a, b, m1, m2):
                    step(v_.tensor_reduce(m1, src, X, ALU.max))
                    step(v_.tensor_tensor(a, src, over(m1, full, 2), ALU.is_equal))
                    step(v_.tensor_tensor(b, a, over(rev, full, 1), ALU.mult))
                    step(v_.tensor_reduce(m2, b, X, ALU.max))
                    step(v_.tensor_tensor(sel, b, over(m2, full, 2), ALU.is_equal))

                if part == 4:
                    largest(kept, g_t[0], g_t[5], g_t[6], t_t[3], t_t[4])
                    step(v_.scalar_tensor_tensor(out=g_t[1], in0=g_t[0], scalar=-BIGGER, in1=kept,
                                                 op0=ALU.mult, op1=ALU.add))
                if part == 5:
                    largest(g_t[1], g_t[3], g_t[5], g_t[6], t_t[5], t_t[6])
                    step(v_.tensor_tensor(g_t[5], g_t[0], g_t[3], ALU.add))
                    c = cc[:, TG * g0:TG * g0 + n]
                    step(v_.tensor_tensor(c[:, :, 2 * E:3 * E], g_t[5], prob, ALU.mult))
                    step(v_.tensor_copy(hi16[:, 0:n], c[:, :, 2 * E:3 * E]))
                    step(v_.tensor_copy(c[:, :, 0:E], hi16[:, 0:n]))
                    v_.tensor_tensor(c[:, :, E:2 * E], c[:, :, 2 * E:3 * E], hi16[:, 0:n], ALU.subtract) \
                      .then_inc(cc_ready, ng)

            def gated(u):
                n, j = unit(u)
                dve.wait_ge(H3_done, u + 1)
                dve.wait_ge(sil_ready, u + 1)
                if u == 0:
                    dve.wait_ge(qm_loaded[G - 1], 16 * HQ)
                if u >= 2:
                    dve.wait_ge(gl_ready, u - 1)
                dst = G32 if j == JE else U
                v_.scalar_tensor_tensor(out=dst[:, u % 2], in0=bank(pair_of(u)[0] + 1),
                                        scalar=pb[:, B_B3 + j:B_B3 + j + 1], in1=sil[:, u % 2],
                                        op0=ALU.add, op1=ALU.mult).then_inc(U_ready, 1)
                if j < JE:
                    dve.wait_ge(U_ready, u + 1)
                    v = n * JE + j
                    dve.wait_ge(spread_done[v % WR], 16 * (P // I) * (v // WR + 1))
                    v_.tensor_tensor(G32[:, u % 2], W[:, v % WR], U[:, u % 2], ALU.mult).then_inc(G_ready, 1)

            def residual(n):
                dve.wait_ge(oT_done, n + 1)
                if n == 0:
                    for hb in range(2):
                        dve.wait_ge(ST_done[hb], T)
                if n >= 2:
                    dve.wait_ge(stored[n % 2], 16 * (n // 2))
                v_.tensor_tensor(ob[:, n % 2], bank(5), xs[:, n * TG:(n + 1) * TG].rearrange("p t c -> p (t c)"),
                                 ALU.add).then_inc(ob_ready, 1)

            for s in range(STEPS):
                for r in round_at(s, "route2"):
                    route(r, 2)
                for i in tile_at(s, "norm"):
                    norm(i)
                for i in tile_at(s, "rotate"):
                    rotate(i)
                for i in tile_at(s, "find_max"):
                    find_max(i)
                for i in tile_at(s, "divide"):
                    divide(i)
                for r in round_at(s, "route4"):
                    route(r, 4)
                for i in tile_at(s, "norm2"):
                    norm2(i)
                for i in tile_at(s, "hi_values"):
                    hi_values(i)
                for g in next_group_at(s, "nstats"):
                    norm_stats(g)
                for r in round_at(s, "route3"):
                    route(r, 3)
                for u in unit_at(s, "gated"):
                    gated(u)
                for r in round_at(s, "route1"):
                    route(r, 1)
                for i in tile_at(s, "lo_values"):
                    lo_values(i)
                for n in chunk_at(s, "residual"):
                    residual(n)
                for g in group_at(s, "read_logits"):
                    read_logits(g)
                for r in round_at(s, "route0"):
                    route(r, 0)
                for i in tile_at(s, "stats2"):
                    stats2(i)
                for r in round_at(s, "route5"):
                    route(r, 5)

        @block.tensor
        def _(pe):
            t_ = nc.tensor

            def turn_tile(i):
                pe.wait_ge(xh_ready, i + 1)
                if i == 0:
                    pe.wait_ge(loaded_a, 16)
                if i % TG == 0:
                    pe.wait_ge(loaded_c[i // TG], 16)
                if i >= 2:
                    pe.wait_ge(xcT_ready, i - 1)
                t_.transpose(bank(i % 2)[:, 0:P], xh[:, i % 2], ident)
                t_.transpose(bank(i % 2)[:, P:2 * P], cs[:, i % (CR * TG)], ident).then_inc(T_done, 1)

            def project(i):
                pe.wait_ge(xcT_ready, i + 1)
                if i >= 2:
                    pe.wait_ge(rot_done, 2 * (i - 1))
                    pe.wait_ge(vl_ready, BT * (i - 1))
                t_.matmul(bank(2 + i % 2)[:, 0:C], xcT[:, i % 2, 0:P], wq, start=True, stop=True)
                t_.matmul(bank(2 + i % 2)[:, C:3 * C], xcT[:, i % 2, P:2 * P], wkv, start=True, stop=True) \
                  .then_inc(qkv_done, 1)

            def turn_stacks(i):
                pe.wait_ge(lo_ready, 2 * (i + 1))
                if i == 0:
                    pe.wait_ge(id16_ready, 1)
                if i >= 2:
                    pe.wait_ge(stk_ready, i - 1)
                for k in range(2 * NS):
                    last = t_.transpose(bank(4 + i % 2).bitcast(F16)[:, P * k:P * k + P],
                                        ex[:, i % 3, P * k:P * k + P], ident16[:])
                last.then_inc(stackT_done, 1)

            def maxima(t, b):
                g, tl = divmod(t, TG)
                if tl == 0 and b == 0:
                    pe.wait_ge(qm_loaded[g], 16 * HQ)
                if t >= 1:
                    pe.wait_ge(mx_ready, BT * (t - 1) + b + 1)
                if b == 1 and tl == 0 and g >= 1:
                    pe.wait_ge(mT_read, g)
                m = tl * BT + b
                for n in range(NP):
                    k, rh = divmod(n, 2)
                    two = QM[:, g % QR, k * TG * BT + m, 2 * rh:2 * rh + 2].rearrange("p h q -> p (h q)")
                    last = t_.matmul(bank(6 + b)[:, S * n:S * n + S], two, stk[:, g, k, S * m:S * m + S],
                                     start=True, stop=True)
                last.then_inc(S_done[b], 1)

            def turn_m(g):
                pe.wait_ge(mx_ready, BT * TG * (g + 1))
                t_.transpose(bank(7)[0:2 * NS * TG * BT, 0:P], mx[:, g % 2], ident).then_inc(mT_done, 1)

            def turn(use):
                pe.wait_ge(*since(use))

            def scores(i, hb):
                g, tl = divmod(i, TG)
                if tl == 0:
                    pe.wait_ge(m_moved[g], 16 * HQ)
                if i == 0:
                    pe.wait_ge(xcT_ready, T)
                else:
                    pe.wait_ge(exp_ready[hb], i)
                for k in (2 * hb, 2 * hb + 1):
                    for b in range(BT):
                        m = tl * BT + b
                        c = HQ * S * (k % 2)
                        last = t_.matmul(bank(hb)[S * b:S * b + S, c:c + HQ * S], stk[:, g, k, S * m:S * m + S],
                                         QM[:, g % QR, k * TG * BT + m].rearrange("p h q -> p (h q)"),
                                         start=True, stop=True)
                last.then_inc(ST_done[hb], 1)

            def values(i):
                pe.wait_ge(pl_ready, i + 1)
                if i == 0:
                    pe.wait_ge(vl_ready, BT * T)
                    pe.wait_ge(stk_ready, T)
                if i >= 1:
                    pe.wait_ge(yt_ready, 4 * i)
                if tiles_before("logits", i + LAG["values"], False) >= TG:
                    pe.wait_ge(log_read, tiles_before("logits", i + LAG["values"], False) // TG)
                for n in range(NP):
                    o = bank(4)[:, VB * n:VB * n + VB]
                    c = slice(P * n, P * n + P)
                    t_.matmul(o, Ph[:, i % RP, c], Vh[:, i, n], start=True, stop=False)
                    t_.matmul(o, Ph[:, i % RP, c], Vl[:, i, n], start=False, stop=False)
                    last = t_.matmul(o, Pl[:, i % 2, c], Vh[:, i, n], start=False, stop=True)
                last.then_inc(pv_done, 1)

            def turn_y(i):
                turn(("y", i))
                pe.wait_ge(yt_ready, 4 * (i + 1))
                t_.transpose(bank(5)[:, 0:P], yt[:, i % RB], ident).then_inc(yT_done, 1)

            def project_out(i):
                if i >= own_w:
                    pe.wait_ge(mT_read, G)
                    pe.wait_ge(x1_ready, i)
                elif i == 0:
                    pe.wait_ge(rot_done, 2 * T)
                    pe.wait_ge(vl_ready, BT * T)
                else:
                    pe.wait_ge(x1_ready, i)
                pe.wait_ge(yT_ready, i + 1)
                if i == 0:
                    pe.wait_ge(loaded_b, 16)
                o = bank(2 if i < own_w else 7)[:, 0:C]
                t_.matmul(o, ident, xs[:, i], start=True, stop=False)
                t_.matmul(o, yT[:, i % RB], wo, start=False, stop=True).then_inc(wo_done, 1)

            def turn_x2(i):
                if i >= own_x:
                    turn(("x", i))
                elif i == 0:
                    pe.wait_ge(rot_done, 2 * T)
                    pe.wait_ge(vl_ready, BT * T)
                else:
                    pe.wait_ge(x2f_ready, i)
                pe.wait_ge(x2n_ready, i + 1)
                t_.transpose(bank(3 if i < own_x else 5)[:, 0:P], x2n[:, i % RB], ident).then_inc(xT_done, 1)

            def logits(i):
                pe.wait_ge(x2l_ready, i + 1)
                pe.wait_ge(wl_ready, 4)
                pe.wait_ge(yt_ready, 4 * tiles_before("values", i + LAG["logits"], True))
                if i % TG == 0 and i >= TG:
                    pe.wait_ge(log_read, i // TG)
                c = slice(P * i, P * i + P)
                o = bank(4)[:, LG + E * (i % TG):LG + E * (i % TG) + E]
                t_.matmul(o, x2h[:, c], gwh[:], start=True, stop=False)
                t_.matmul(o, x2h[:, c], gwl[:], start=False, stop=False)
                t_.matmul(o, x2l[:, c], gwh[:], start=False, stop=True).then_inc(log_done, 1)

            def split(o, n, j, mh, ml, start=True, stop=True):
                w = slice(P * j, P * j + P)
                t_.matmul(o, wh[n][:, w], mh, start=start, stop=False)
                t_.matmul(o, wh[n][:, w], ml, start=False, stop=False)
                return t_.matmul(o, wl[n][:, w], mh, start=False, stop=stop)

            def up(u):
                n, j = unit(u)
                c = slice(CH * n, CH * n + CH)
                pair, last = pair_of(u)
                if pair == 0 and last < 0:
                    for hb in range(2):
                        pe.wait_ge(exp_ready[hb], T)
                if pair == 2 and last < 0:
                    pe.wait_ge(x1_ready, own_w)
                    pe.wait_ge(x2f_ready, own_x)
                    pe.wait_ge(rot_done, 2 * T)
                    pe.wait_ge(vl_ready, BT * T)
                if j == JE:
                    pe.wait_ge(x2l_ready, TG * (n + 1))
                if last >= 0:
                    pe.wait_ge(sil_ready, last + 1)
                split(bank(pair), 0, j, x2h[:, c], x2l[:, c]).then_inc(H1_done, 1)
                if last >= 0:
                    pe.wait_ge(U_ready, last + 1)
                split(bank(pair + 1), 1, j, x2h[:, c], x2l[:, c]).then_inc(H3_done, 1)

            def down(u):
                n, j = unit(u)
                pe.wait_ge(gl_ready, u + 1)
                if j == JE and n == 0:
                    pe.wait_ge(mx_ready, BT * T)
                elif j == JE and n >= 2:
                    pe.wait_ge(yo_ready, n - 1)
                if j == JE and n == 1:
                    pe.wait_ge(mT_read, G)
                    pe.wait_ge(x1_ready, T)
                if j == 0:
                    pe.wait_ge(cT_ready, n + 1)
                split(bank(6 + n % 2), 2, j, Gh[:, u % 3], Gl[:, u % 2],
                      start=j == JE, stop=j == JE - 1) \
                    .then_inc(Y_part, 1)
                if j == 0:
                    t_.matmul(bank(6 + n % 2), b2h[:], cT[:, n % 2], start=False, stop=False)
                    t_.matmul(bank(6 + n % 2), b2l[:], cT[:, n % 2], start=False, stop=False)

            def turn_c(n):
                turn(("c", n))
                pe.wait_ge(cc_ready, n + 1)
                for t in range(TG):
                    last = t_.transpose(bank(5)[0:3 * E, P * t:P * t + P], cc[:, n * TG + t], ident)
                last.then_inc(cT_done, 1)

            def turn_out(n):
                turn(("o", n))
                pe.wait_ge(yo_ready, n + 1)
                for t in range(TG):
                    last = t_.transpose(bank(5)[:, P * t:P * t + P], yo[:, n % 2, P * t:P * t + P], ident)
                last.then_inc(oT_done, 1)

            for s in range(STEPS):
                for i in tile_at(s, "scores1"):
                    scores(i, 1)
                for i in tile_at(s, "maxima0"):
                    maxima(i, 0)
                for u in unit_at(s, "up"):
                    up(u)
                for i in tile_at(s, "scores0"):
                    scores(i, 0)
                for i in tile_at(s, "maxima1"):
                    maxima(i, 1)
                for u in unit_at(s, "down"):
                    down(u)
                for i in tile_at(s, "values"):
                    values(i)
                for i in tile_at(s, "turn_tile"):
                    turn_tile(i)
                for i in tile_at(s, "project"):
                    project(i)
                for i in tile_at(s, "turn_y"):
                    turn_y(i)
                for n in chunk_at(s, "turn_out"):
                    turn_out(n)
                for n in experts_at(s, "turn_c"):
                    turn_c(n)
                for i in tile_at(s, "project_out"):
                    project_out(i)
                for i in tile_at(s, "turn_stacks"):
                    turn_stacks(i)
                for i in tile_at(s, "turn_x2"):
                    turn_x2(i)
                for g in group_at(s, "turn_m"):
                    turn_m(g)
                for i in tile_at(s, "logits"):
                    logits(i)


def kernel(x, ctx_1024, L0_xattn_Wq, L0_xattn_Wk, L0_xattn_Wv, L0_xattn_Wo, L0_ffn_gate_w, L0_ffn_gate_b,
           L0_ffn_We1, L0_ffn_be1, L0_ffn_We2, L0_ffn_be2, L0_ffn_We3, L0_ffn_be3, L0_ffn_ws1, L0_ffn_bs1,
           L0_ffn_ws2, L0_ffn_bs2, L0_ffn_ws3, L0_ffn_bs3):
    import numpy as np
    import concourse.bacc as bacc
    from concourse.bass_utils import run_bass_kernel_spmd

    f = lambda a: np.asarray(a)
    freqs = 1.0 / 10000.0 ** (np.arange(0, C, 2, dtype=np.float32) / C)
    ang = np.outer(np.arange(S, dtype=np.float32), freqs.astype(np.float32)).astype(np.float32)
    cosv = np.tile(np.repeat(np.cos(ang), 2, 1), (BT, 1))
    sinv = np.tile(np.repeat(np.sin(ang), 2, 1) * np.tile([-1.0, 1.0], C // 2), (BT, 1))
    scale = 1.0 / np.sqrt(D)
    cos = np.concatenate([cosv * scale, cosv], 1).astype(np.float32)
    sin = np.concatenate([sinv * scale, sinv], 1).astype(np.float32)
    ident = np.eye(P, dtype=np.float32)
    below = np.tile(np.tril(np.ones((NG, NG), np.float32), -1).reshape(1, -1), (P, 1))
    rev = np.tile(np.arange(E, 0, -1, dtype=np.float32), (P, 1))

    col = lambda be, bs: np.concatenate([f(be).reshape(JE, P).T, f(bs).reshape(P, 1)], 1)
    pack_a = np.concatenate([f(L0_xattn_Wq).T, f(L0_xattn_Wk).T, f(L0_xattn_Wv).T, cos, sin, ident], 1)
    pack_b = np.concatenate([f(L0_xattn_Wo).T, f(L0_ffn_gate_w).T, np.tile(f(L0_ffn_gate_b).reshape(1, E), (P, 1)),
                             col(L0_ffn_be1, L0_ffn_bs1), col(L0_ffn_be3, L0_ffn_bs3),
                             f(L0_ffn_bs2).reshape(P, 1), below, rev], 1)
    pack_k = np.tile(f(L0_ffn_be2), (2, 1))
    up = lambda we, ws: np.concatenate([f(we).transpose(1, 0, 2).reshape(C, E * I), f(ws)], 1)
    w2 = np.concatenate([f(L0_ffn_We2).reshape(JE, P, C).transpose(1, 0, 2).reshape(P, JE * C), f(L0_ffn_ws2)], 1)
    arrays = {
        "in_x": f(x).reshape(TOK, C), "in_ctx": f(ctx_1024).reshape(TOK, C), "in_a": pack_a, "in_b": pack_b,
        "in_k": pack_k, "in_w1": up(L0_ffn_We1, L0_ffn_ws1), "in_w3": up(L0_ffn_We3, L0_ffn_ws3), "in_w2": w2,
    }
    arrays = {k: np.ascontiguousarray(v) for k, v in arrays.items()}
    nc = bacc.Bacc("TRN2", target_bir_lowering=False, num_devices=1)
    args = [nc.dram_tensor(k, v.shape, mybir.dt.from_np(v.dtype), kind="ExternalInput").ap()
            for k, v in arrays.items()]
    args.append(nc.dram_tensor("out", (TOK, C), F32, kind="ExternalOutput").ap())
    program(nc, *args)
    r = run_bass_kernel_spmd(nc, [arrays], core_ids=[0])
    return r.results[0]["out"].reshape(B, S, C)
```
